# Optimizing a Trainium2 kernel written in Bass

```python
import numpy as np
import jax
import jax.numpy as jnp

def _softmax(x, axis=-1):
    return jax.nn.softmax(x, axis=axis)

def _gelu(x):
    return jax.nn.gelu(x, approximate=True)

def _silu(x):
    return jax.nn.silu(x)

def _sigmoid(x):
    return jax.nn.sigmoid(x)

def _layernorm(x, axis=-1, eps=1e-05):
    m = jnp.mean(x, axis=axis, keepdims=True)
    v = jnp.var(x, axis=axis, keepdims=True)
    return (x - m) / jnp.sqrt(v + eps)

def _scatter_add(tgt, idx, src, axis=0):
    return tgt.at[idx].add(src)

def _segment_sum(src, seg, n):
    return jax.ops.segment_sum(src, seg, n)
kernel_name = 'mk_adj_preln_d4_adj_r2_3e9f16'

def setup_inputs(seed: int=0):
    np.random.seed(seed)
    _w = jnp.asarray

    def _rec_inputs():
        import jax
        import jax.numpy as jnp
        _gk = jax.random.key(seed)
        x = 7.22e-05 + 1 * jax.random.normal(jax.random.fold_in(_gk, 1), (128, 128, 256), jnp.float32)
        _a = jax.random.bernoulli(jax.random.fold_in(_gk, 2), 0.03125, (128, 128))
        _a = jnp.logical_or(_a, jnp.swapaxes(_a, -1, -2))
        _a = jnp.logical_or(_a, jnp.eye(128, dtype=bool))
        adj = _a.astype(jnp.int32)
        return (x, adj)
    x, adj = _rec_inputs()

    def _L0_gnn_setup():
        import jax, jax.numpy as jnp
        import numpy as np
        LEAKY_ALPHA = 0.01
        NEG_INF = -1000000000.0
        LN_EPS = 1e-05

        def _gat_heads(x, adj, W, a):
            O = W.shape[-1]
            Wh = jnp.einsum('bnf,hfo->bhno', x, W)
            f1 = jnp.einsum('bhno,ho->bhn', Wh, a[:, :O])
            f2 = jnp.einsum('bhno,ho->bhn', Wh, a[:, O:])
            e = f1[:, :, :, None] + f2[:, :, None, :]
            e = jnp.where(e > 0, e, LEAKY_ALPHA * e)
            e = jnp.where(adj[None, None] > 0, e, NEG_INF)
            attn = jax.nn.softmax(e, axis=-1)
            return jnp.einsum('bhnm,bhmo->bhno', attn, Wh)
        key = jax.random.key(seed)
        ks = jax.random.split(key, 10)
        B, N, F_in, F_hid, H, F_out, D_ff = (8, 1024, 256, 256, 4, 256, 256)
        s = 0.05
        return {'enc_inputs': jax.random.normal(ks[0], (B, N, F_in), jnp.float32), 'adj': jax.random.randint(ks[1], (N, N), 0, 2, jnp.int32), 'W_heads': jax.random.normal(ks[2], (H, F_in, F_hid), jnp.float32) * s, 'a_heads': jax.random.normal(ks[3], (H, 2 * F_hid), jnp.float32) * s, 'W_out': jax.random.normal(ks[4], (H * F_hid, F_out), jnp.float32) * s, 'a_out': jax.random.normal(ks[5], (2 * F_out,), jnp.float32) * s, 'w1': jax.random.normal(ks[6], (F_out, D_ff), jnp.float32) * s, 'b1': jnp.zeros((D_ff,), jnp.float32), 'w2': jax.random.normal(ks[7], (D_ff, F_out), jnp.float32) * s, 'b2': jnp.zeros((F_out,), jnp.float32), 'ln_gamma': jnp.ones((F_out,), jnp.float32), 'ln_beta': jnp.zeros((F_out,), jnp.float32)}
    _L0_gnn_all = _L0_gnn_setup()
    _L0_gnn_in = {k: v for k, v in _L0_gnn_all.items() if k in ('W_heads', 'a_heads', 'W_out', 'a_out', 'w1', 'b1', 'w2', 'b2', 'ln_gamma', 'ln_beta')}
    del _L0_gnn_all

    def _L1_gnn_setup():
        import jax, jax.numpy as jnp
        import numpy as np
        D_MODEL = 256
        NUM_HEADS = 8
        D_HEAD = D_MODEL // NUM_HEADS
        B, N = (4, 1024)
        key = jax.random.key(seed)
        ks = jax.random.split(key, 10)
        s = 1.0 / np.sqrt(D_MODEL)
        inp = {'h': jax.random.normal(ks[0], (B, N, D_MODEL), dtype=jnp.float32), 'adj': jax.random.randint(ks[1], (N, N), 0, 2, dtype=jnp.int32), 'Wq': jax.random.uniform(ks[2], (D_MODEL, D_MODEL), jnp.float32, -s, s), 'bq': jax.random.uniform(ks[3], (D_MODEL,), jnp.float32, -s, s), 'Wk': jax.random.uniform(ks[4], (D_MODEL, D_MODEL), jnp.float32, -s, s), 'bk': jax.random.uniform(ks[5], (D_MODEL,), jnp.float32, -s, s), 'Wv': jax.random.uniform(ks[6], (D_MODEL, D_MODEL), jnp.float32, -s, s), 'bv': jax.random.uniform(ks[7], (D_MODEL,), jnp.float32, -s, s), 'Wo': jax.random.uniform(ks[8], (D_MODEL, D_MODEL), jnp.float32, -s, s), 'bo': jax.random.uniform(ks[9], (D_MODEL,), jnp.float32, -s, s)}
        return inp
    _L1_gnn_all = _L1_gnn_setup()
    _L1_gnn_in = {k: v for k, v in _L1_gnn_all.items() if k in ('Wq', 'bq', 'Wk', 'bk', 'Wv', 'bv', 'Wo', 'bo')}
    del _L1_gnn_all

    def _L2_gnn_setup():
        import jax, jax.numpy as jnp
        import numpy as np
        B, K, DIN, DOUT = (32, 64, 256, 256)
        key = jax.random.key(seed)
        k1, k2, k3, k4 = jax.random.split(key, 4)
        x = jax.random.normal(k1, (B, K, DIN), dtype=jnp.float32)
        adj = jax.random.randint(k2, (K, K), 0, 2, dtype=jnp.int32)
        W = jax.random.normal(k3, (DOUT, 2 * DIN), dtype=jnp.float32) * 0.02
        b = jax.random.normal(k4, (DOUT,), dtype=jnp.float32) * 0.02
        return {'x': x, 'adj': adj, 'W': W, 'b': b}
    _L2_gnn_all = _L2_gnn_setup()
    _L2_gnn_in = {k: v for k, v in _L2_gnn_all.items() if k in ('W', 'b')}
    del _L2_gnn_all

    def _L3_gnn_setup():
        import jax, jax.numpy as jnp
        import numpy as np
        B, N, F, F1 = (512, 75, 256, 128)
        NEG = -1000000000.0
        ALPHA = 0.2
        key = jax.random.key(seed)
        k1, k2, k3, k4 = jax.random.split(key, 4)
        X = jax.random.normal(k1, (B, N, F), dtype=jnp.float32)
        A = jax.random.randint(k2, (N, N), 0, 2, dtype=jnp.int32)
        W = jax.random.normal(k3, (F, F1), dtype=jnp.float32) * (1.0 / np.sqrt(F))
        a = jax.random.normal(k4, (2, F1, 1), dtype=jnp.float32) * (1.0 / np.sqrt(F1))
        return {'X': X, 'A': A, 'W': W, 'a': a}
    _L3_gnn_all = _L3_gnn_setup()
    _L3_gnn_in = {k: v for k, v in _L3_gnn_all.items() if k in ('W', 'a')}
    del _L3_gnn_all
    return {'x': x, 'adj': adj, 'L0_gnn_W_heads': _L0_gnn_in['W_heads'], 'L0_gnn_a_heads': _L0_gnn_in['a_heads'], 'L0_gnn_W_out': _L0_gnn_in['W_out'], 'L0_gnn_a_out': _L0_gnn_in['a_out'], 'L0_gnn_w1': _L0_gnn_in['w1'], 'L0_gnn_b1': _L0_gnn_in['b1'], 'L0_gnn_w2': _L0_gnn_in['w2'], 'L0_gnn_b2': _L0_gnn_in['b2'], 'L0_gnn_ln_gamma': _L0_gnn_in['ln_gamma'], 'L0_gnn_ln_beta': _L0_gnn_in['ln_beta'], 'L1_gnn_Wq': _L1_gnn_in['Wq'], 'L1_gnn_bq': _L1_gnn_in['bq'], 'L1_gnn_Wk': _L1_gnn_in['Wk'], 'L1_gnn_bk': _L1_gnn_in['bk'], 'L1_gnn_Wv': _L1_gnn_in['Wv'], 'L1_gnn_bv': _L1_gnn_in['bv'], 'L1_gnn_Wo': _L1_gnn_in['Wo'], 'L1_gnn_bo': _L1_gnn_in['bo'], 'L2_gnn_W': _L2_gnn_in['W'], 'L2_gnn_b': _L2_gnn_in['b'], 'L3_gnn_W': _L3_gnn_in['W'], 'L3_gnn_a': _L3_gnn_in['a']}

def reference(x, adj, L0_gnn_W_heads, L0_gnn_a_heads, L0_gnn_W_out, L0_gnn_a_out, L0_gnn_w1, L0_gnn_b1, L0_gnn_w2, L0_gnn_b2, L0_gnn_ln_gamma, L0_gnn_ln_beta, L1_gnn_Wq, L1_gnn_bq, L1_gnn_Wk, L1_gnn_bk, L1_gnn_Wv, L1_gnn_bv, L1_gnn_Wo, L1_gnn_bo, L2_gnn_W, L2_gnn_b, L3_gnn_W, L3_gnn_a):
    import jax
    import jax.numpy as jnp

    def _L0_gnn_ref(enc_inputs, adj, W_heads, a_heads, W_out, a_out, w1, b1, w2, b2, ln_gamma, ln_beta):
        import jax, jax.numpy as jnp
        import numpy as np
        LEAKY_ALPHA = 0.01
        NEG_INF = -1000000000.0
        LN_EPS = 1e-05

        def _gat_heads(x, adj, W, a):
            O = W.shape[-1]
            Wh = jnp.einsum('bnf,hfo->bhno', x, W)
            f1 = jnp.einsum('bhno,ho->bhn', Wh, a[:, :O])
            f2 = jnp.einsum('bhno,ho->bhn', Wh, a[:, O:])
            e = f1[:, :, :, None] + f2[:, :, None, :]
            e = jnp.where(e > 0, e, LEAKY_ALPHA * e)
            e = jnp.where(adj[None, None] > 0, e, NEG_INF)
            attn = jax.nn.softmax(e, axis=-1)
            return jnp.einsum('bhnm,bhmo->bhno', attn, Wh)
        B, N, _ = enc_inputs.shape
        h = jax.nn.elu(_gat_heads(enc_inputs, adj, W_heads, a_heads))
        h = jnp.transpose(h, (0, 2, 1, 3)).reshape(B, N, -1)
        out = _gat_heads(h, adj, W_out[None], a_out[None])[:, 0]
        out = jax.nn.elu(out)
        ffn = jnp.maximum(out @ w1 + b1, 0.0) @ w2 + b2
        y = ffn + out
        mu = jnp.mean(y, axis=-1, keepdims=True)
        var = jnp.var(y, axis=-1, keepdims=True)
        return (y - mu) / jnp.sqrt(var + LN_EPS) * ln_gamma + ln_beta

    def _L1_gnn_ref(h, adj, Wq, bq, Wk, bk, Wv, bv, Wo, bo):
        import jax, jax.numpy as jnp
        import numpy as np
        D_MODEL = 256
        NUM_HEADS = 8
        D_HEAD = D_MODEL // NUM_HEADS
        B, N = (4, 1024)
        b, n, _ = h.shape

        def split_heads(x):
            return x.reshape(b, n, NUM_HEADS, D_HEAD).transpose(0, 2, 1, 3)
        q = split_heads(h @ Wq.T + bq)
        k = split_heads(h @ Wk.T + bk)
        v = split_heads(h @ Wv.T + bv)
        scale = 1.0 / np.sqrt(D_HEAD)
        scores = jnp.einsum('bhqd,bhkd->bhqk', q, k) * scale
        mask = (adj == 0)[None, None, :, :]
        scores = jnp.where(mask, -jnp.inf, scores)
        attn = jax.nn.softmax(scores, axis=-1)
        out = jnp.einsum('bhqk,bhkd->bhqd', attn, v)
        out = out.transpose(0, 2, 1, 3).reshape(b, n, D_MODEL)
        return out @ Wo.T + bo

    def _L2_gnn_ref(x, adj, W, b):
        import jax, jax.numpy as jnp
        import numpy as np
        B, K, DIN, DOUT = (32, 64, 256, 256)
        Din = x.shape[-1]
        Wi, Wj = (W[:, :Din], W[:, Din:])
        mi = jnp.einsum('bkd,od->bko', x, Wi)
        mj = jnp.einsum('bkd,od->bko', x, Wj)
        a = adj.astype(x.dtype)
        deg = a.sum(axis=1)
        out = deg[None, :, None] * (mi + b) + jnp.einsum('ij,bjo->bio', a, mj)
        return out

    def _L3_gnn_ref(X, A, W, a):
        import jax, jax.numpy as jnp
        import numpy as np
        B, N, F, F1 = (512, 75, 256, 128)
        NEG = -1000000000.0
        ALPHA = 0.2
        h = jnp.einsum('bnf,fo->bno', X, W)
        att_self = jnp.einsum('bno,od->bnd', h, a[0])
        att_neigh = jnp.einsum('bno,od->bnd', h, a[1])
        e = att_self + jnp.swapaxes(att_neigh, 1, 2)
        e = jax.nn.leaky_relu(e, ALPHA)
        adj = A.astype(h.dtype)
        e = e + NEG * (1.0 - adj)[None, :, :]
        alpha = jax.nn.softmax(e, axis=-1)
        out = jnp.einsum('bij,bjo->bio', alpha, h)
        return jnp.concatenate([out, h], axis=-1)
    h = jnp.maximum(_layernorm(x, axis=-1), 0.0)
    x = x + _L0_gnn_ref(h, adj, L0_gnn_W_heads, L0_gnn_a_heads, L0_gnn_W_out, L0_gnn_a_out, L0_gnn_w1, L0_gnn_b1, L0_gnn_w2, L0_gnn_b2, L0_gnn_ln_gamma, L0_gnn_ln_beta)
    h = jnp.maximum(_layernorm(x, axis=-1), 0.0)
    x = x + _L1_gnn_ref(h, adj, L1_gnn_Wq, L1_gnn_bq, L1_gnn_Wk, L1_gnn_bk, L1_gnn_Wv, L1_gnn_bv, L1_gnn_Wo, L1_gnn_bo)
    h = jnp.maximum(_layernorm(x, axis=-1), 0.0)
    x = x + _L2_gnn_ref(h, adj, L2_gnn_W, L2_gnn_b)
    h = jnp.maximum(_layernorm(x, axis=-1), 0.0)
    x = x + _L3_gnn_ref(h, adj, L3_gnn_W, L3_gnn_a)
    return x

_drawn_inputs = setup_inputs


def setup_inputs(seed=0):
    import zlib

    import numpy as np

    out = dict(_drawn_inputs(seed))
    spreads = {'L0_gnn_b1': (0.0, 0.1),
     'L0_gnn_b2': (0.0, 0.1),
     'L0_gnn_ln_gamma': (1.0, 0.2),
     'L0_gnn_ln_beta': (0.0, 0.1)}
    factors = {'L0_gnn_a_out': 3.944,
     'L1_gnn_Wq': 8.0,
     'L1_gnn_bq': 42.668,
     'L1_gnn_Wk': 8.0,
     'L1_gnn_bk': 64.0,
     'L1_gnn_bv': 4.41,
     'L3_gnn_a': 8.0}
    for name, (base, spread) in spreads.items():
        noise = np.random.default_rng([zlib.crc32(name.encode()), seed]).standard_normal(out[name].shape)
        drawn = base * np.exp(spread * noise) if base else spread * noise
        out[name] = jnp.asarray(drawn.astype(out[name].dtype))
    for name, factor in factors.items():
        out[name] = (out[name] * factor).astype(out[name].dtype)
    return out
```

```python
import concourse.bass as bass
from concourse import mybir
from contextlib import ExitStack

ALU = mybir.AluOpType
ACT = mybir.ActivationFunctionType
AX = mybir.AxisListType
F32 = mybir.dt.float32
BF16 = mybir.dt.bfloat16
I32 = mybir.dt.int32

EPS = 1e-5
MASKED = -1e11
SLOPE_L0 = 0.01
SLOPE_L3 = 0.2
HEADS_L1 = 8
SLOTS = 8

CHAINS = "ABCDE"

PE_ORDER = """
B_o D_zT C_fT D_qkv A_zT E_zT C_s A_wh D_s E_m A_fT C_pT B_hT C_o E_am A_s C_hT E_zT3 D_pT B_wh E_h C_hid E_fT
D_o E_s C_ffn D_oT A_pT D_out E_pT E_o
""".split()
ACT_ORDER = """
D_hT B_exp A_hT D_qc E_hT C_slope C_exp A_whc_hi A_whc_lo C_attn D_exp C_oexp B_hTc_lo A_slope E_hT3 C_hTc
D_pTc_lo A_exp B_whc E_hc C_hidc E_slope D_oTc E_exp A_attn E_attn
""".split()
DVE_ORDER = """
D_stats A_stats D_z E_stats A_z C_fTc E_z B_h D_kc D_vc C_max A_fcopy C_recip D_max E_mj A_fTc B_hTc_hi E_x3
C_h E_z3 A_max D_pTc_hi A_norm E_fTc D_on E_max C_y E_recip C_x1 D_x2 E_left
""".split()
POOL_ORDER = """
C_xb D_rstd A_rstd D_xb E_rstd E_rstd3 C_hb E_right C_rstd
""".split()

STEP_SEMAPHORES = """
A_stats A_moments A_var A_rstd A_z A_zT A_hT A_f A_fcopy A_wh_hi A_wh_lo A_whc_hi A_whc_lo A_fT A_fTc A_s A_slope A_leaky
A_max A_shift A_exp A_sum A_recip A_norm A_pT A_attn
B_o B_exp B_min B_h B_hT B_hTc_lo B_hTc_hi B_wh B_whc
C_fT C_fTc C_s C_slope C_leaky C_max C_exp C_recip C_pT C_attn C_o C_oexp C_min C_h C_hb C_hT C_hTc C_hid C_hidc C_ffn C_y
C_stats C_moments C_var C_rstd C_xb C_g C_x1
D_stats D_moments D_var D_rstd D_z D_xb D_zT D_hT D_q D_kv D_qc D_kc D_vc D_s D_max D_shift D_exp D_pT D_pTc_lo D_pTc_hi
D_o D_recip D_on D_oT D_oTc D_out D_x2
E_stats E_moments E_var E_rstd E_z E_zT E_hT E_m E_mj E_xm E_am E_x3
E_stats3 E_moments3 E_var3 E_rstd3 E_z3 E_zT3 E_hT3 E_h E_hc E_fT E_fTc E_s E_slope E_leaky E_max E_exp E_recip E_pT E_attn
E_o E_left E_right
""".split()


def gnn_stack(nc, x, adj, w_heads, a_heads, w_out, a_out, w1, b1, w2, b2, gamma, beta,
              wqT, bq, wkT, bk, wvT, bv, woT, bo, wijT, b_l2, w_l3, a_l3, out):
    GRAPHS, N, D = x.shape
    P = 128
    assert N == P and D == 2 * P
    K = D // P
    H0 = w_heads.shape[0]
    HD = H0 * D
    KH = HD // P
    DH = D // HEADS_L1
    HPC = P // DH
    F3 = w_l3.shape[1]
    SCALE = float(DH) ** -0.5

    with ExitStack() as ctx:
        def sb(name, shape, dt=F32):
            return ctx.enter_context(nc.sbuf_tensor(name, shape, dt))

        def ps(name, shape):
            return ctx.enter_context(nc.psum_tensor(name, shape, F32))

        def sem(name):
            return ctx.enter_context(nc.semaphore(name))

        ident = sb("ident", [P, P])
        ident_bf = sb("ident_bf", [P, P], BF16)
        rows = sb("rows", [2 * H0, 2 * H0, P])
        head_of = sb("head_of", [P, HPC])
        adj_i = sb("adj_i", [P, P], I32)
        adj_f = sb("adj_f", [P, P])
        adjT = sb("adjT", [P, P])
        mask = sb("mask", [P, P], BF16)
        deg = sb("deg", [P, 1])
        minus_half = sb("minus_half", [P, 1])
        wh_w = sb("wh_w", [P, K, H0, D])
        wa_w = sb("wa_w", [P, K, 2 * H0])
        a0_b = sb("a0_b", [P, H0, 2 * D])
        wout_w = sb("wout_w", [P, KH, D + 2])
        aout_b = sb("aout_b", [P, 2 * D])
        w1_w = sb("w1_w", [P, K, D])
        w2_w = sb("w2_w", [P, K, D])
        b1_c = sb("b1_c", [P, K])
        b2_b = sb("b2_b", [P, D])
        gamma_b = sb("gamma_b", [P, D])
        beta_b = sb("beta_b", [P, D])
        wq_w = sb("wq_w", [P, K, D])
        wk_w = sb("wk_w", [P, K, D])
        wv_w = sb("wv_w", [P, K, D])
        wo_w = sb("wo_w", [P, K, D])
        bq_c = sb("bq_c", [P, K])
        bk_c = sb("bk_c", [P, K])
        bv_b = sb("bv_b", [P, D])
        bo_b = sb("bo_b", [P, D])
        wij_w = sb("wij_w", [P, K, 2 * D])
        bl2_b = sb("bl2_b", [P, D])
        w3_w = sb("w3_w", [P, K, F3 + 2])
        a3_b = sb("a3_b", [P, 2 * F3])
        products = sb("products", [P, D])

        xs = sb("xs", [P, SLOTS, D])

        A_st, A_mv, A_ve, A_rs = sb("A_st", [P, 6]), sb("A_mv", [P, 2]), sb("A_ve", [P, 1]), sb("A_rs", [P, 1])
        A_z, A_hT = sb("A_z_t", [P, D]), sb("A_hT_t", [P, D])
        A_f, A_fT = sb("A_f_t", [P, 2 * H0]), sb("A_fT_t", [2 * H0, P])
        A_l = sb("A_l", [P, H0, P])
        A_m, A_sum, A_rec = sb("A_m", [P, H0]), sb("A_sum_t", [P, H0]), sb("A_rec", [P, H0])
        whs = sb("whs", [P, H0, D])
        attnT = sb("attnT", [P, H0, P])
        B_e = sb("B_e", [P, HD])
        B_hT = sb("B_hT_t", [P, KH, P])
        wh2 = sb("wh2", [P, D + 2])
        C_fT = sb("C_fT_t", [2, P])
        C_l, C_aT = sb("C_l", [P, P]), sb("C_aT", [P, P])
        C_m, C_sum, C_rec = sb("C_m", [P, 1]), sb("C_sum", [P, 1]), sb("C_rec", [P, 1])
        C_e, C_h, C_hb, C_hT, C_hid = (sb(n, [P, D]) for n in ("C_e", "C_h_t", "C_hb_t", "C_hT_t", "C_hid_t"))
        C_y, C_g = sb("C_y_t", [P, D]), sb("C_g_t", [P, D])
        C_st, C_mv, C_ve, C_rs = sb("C_st", [P, 6]), sb("C_mv", [P, 2]), sb("C_ve", [P, 1]), sb("C_rs", [P, 1])
        D_st, D_mv, D_ve, D_rs = sb("D_st", [P, 6]), sb("D_mv", [P, 2]), sb("D_ve", [P, 1]), sb("D_rs", [P, 1])
        D_z, D_hT = sb("D_z_t", [P, D]), sb("D_hT_t", [P, D])
        D_q = sb("D_q_t", [P, K, P])
        D_k = sb("D_k_t", [P, K, HPC, P])
        D_v = sb("D_v_t", [P, HEADS_L1, DH + 1])
        D_s = sb("D_s_t", [P, HEADS_L1, P])
        D_pT = sb("D_pT_t", [P, HEADS_L1, P])
        D_m, D_rec = sb("D_m", [P, HEADS_L1]), sb("D_rec", [P, HEADS_L1])
        D_o, D_oT = sb("D_o_t", [P, D]), sb("D_oT_t", [P, D])
        E_st, E_mv, E_ve, E_rs = sb("E_st", [P, 6]), sb("E_mv", [P, 2]), sb("E_ve", [P, 1]), sb("E_rs", [P, 1])
        E_z, E_hT = sb("E_z_t", [P, D]), sb("E_hT_t", [P, D])
        E_mj = sb("E_mj_t", [P, D])
        E_h = sb("E_h_t", [P, F3 + 2])
        E_fT = sb("E_fT_t", [2, P])
        E_l, E_aT = sb("E_l", [P, P]), sb("E_aT", [P, P])
        E_m, E_sum, E_rec = sb("E_m_t", [P, 1]), sb("E_sum", [P, 1]), sb("E_rec", [P, 1])

        pA = ps("pA", [P, 2, 512])
        pB = ps("pB", [P, 2, 512])
        pC = ps("pC", [P, 512])
        pD = ps("pD", [P, 2, 512])
        pE = ps("pE", [P, 512])

        S = {name: sem(name) for name in STEP_SEMAPHORES}
        weights_loaded = sem("weights_loaded")
        zeroed = sem("zeroed")
        consts_built = sem("consts_built")
        adj_ready = sem("adj_ready")
        adjT_done = sem("adjT_done")
        deg_ready = sem("deg_ready")
        dve_setup = sem("dve_setup")
        x_loaded = sem("x_loaded")
        stored = sem("stored")

        def slot(g):
            return xs[:, g % SLOTS, :]

        def done(eng, name, g):
            eng.wait_ge(S[name], g + 1)

        def done_apart(eng, name, g):
            eng.wait_ge(consts_built, 4)
            done(eng, name, g)

        def done_before(eng, name, g):
            if not (isinstance(g, int) and g == 0):
                eng.wait_ge(S[name], g)

        def rounds(eng, order, steps):
            def one(i):
                for name in order:
                    g = i - CHAINS.index(name[0])
                    if not isinstance(g, int) or 0 <= g < GRAPHS:
                        steps[name](g)
            for i in range(len(CHAINS)):
                one(i)
            with eng.Fori(len(CHAINS), GRAPHS) as i:
                one(i)
            for i in range(GRAPHS, GRAPHS + len(CHAINS) - 1):
                one(i)

        small_loads = [
            (b1_c[:, :], b1),
            (bq_c[:, :], bq),
            (bk_c[:, :], bk),
            (b2_b[:, :], b2.partition_broadcast(P)),
            (gamma_b[:, :], gamma.partition_broadcast(P)),
            (beta_b[:, :], beta.partition_broadcast(P)),
            (bv_b[:, :], bv.partition_broadcast(P)),
            (bo_b[:, :], bo.partition_broadcast(P)),
            (bl2_b[:, :], b_l2.partition_broadcast(P)),
            (aout_b[:, :], a_out.partition_broadcast(P)),
            (a3_b[:, :], a_l3.rearrange("t f one -> (t f one)").partition_broadcast(P)),
            (a0_b[:, :, :].rearrange("p h d -> p (h d)"), a_heads.rearrange("h d -> (h d)").partition_broadcast(P)),
        ]
        loads = [(adj_i[:, :], adj)]
        loads += [(wh_w[:, c, :, :], w_heads[:, c * P:(c + 1) * P, :].rearrange("h p d -> p h d")) for c in range(K)]
        loads += [(wout_w[:, :, 0:D], w_out.rearrange("(k p) d -> p k d", p=P)),
                  (w3_w[:, :, 0:F3], w_l3.rearrange("(k p) d -> p k d", p=P))]
        loads += [(t[:, :, :], w.rearrange("(k p) d -> p k d", p=P))
                  for t, w in ((w1_w, w1), (w2_w, w2), (wq_w, wqT), (wk_w, wkT), (wv_w, wvT), (wo_w, woT), (wij_w, wijT))]
        LOADED = 16 * (len(loads) + len(small_loads))

        block = ctx.enter_context(nc.Block())

        @block.sync
        def _(sp):
            for dst, src in loads:
                sp.dma_start(dst, src).then_inc(weights_loaded, 16)

            def load(g, freed):
                if freed:
                    sp.wait_ge(stored, 16 * (g - SLOTS + 1))
                if not (isinstance(g, int) and g == 0):
                    sp.wait_ge(x_loaded, 16 * g)
                sp.dma_start(slot(g), x[g]).then_inc(x_loaded, 16)

            def store(g):
                done(sp, "E_left", g)
                done(sp, "E_right", g)
                sp.dma_start(out[g], slot(g)).then_inc(stored, 16)

            for g in range(SLOTS):
                load(g, freed=False)
            with sp.Fori(0, GRAPHS - SLOTS) as g:
                store(g)
                load(g + SLOTS, freed=True)
            for g in range(GRAPHS - SLOTS, GRAPHS):
                sp.wait_ge(stored, 16 * g)
                store(g)
            sp.wait_ge(stored, 16 * GRAPHS)

        @block.gpsimd
        def _(pool):
            pool.memset(ident[:, :], 0.0).then_inc(zeroed, 1)
            pool.memset(rows[:, :, :], 0.0).then_inc(zeroed, 1)
            pool.memset(head_of[:, :], 1.0).then_inc(zeroed, 1)
            pool.memset(minus_half[:, :], -0.5).then_inc(zeroed, 1)
            pool.wait_ge(zeroed, 4)
            pool.affine_select(out=ident[:, :], in_=ident[:, :], compare_op=ALU.not_equal, fill=1.0, base=0,
                               pattern=[[-1, P]], channel_multiplier=1).then_inc(consts_built, 1)
            pool.affine_select(out=rows[:, :, :], in_=rows[:, :, :], compare_op=ALU.not_equal, fill=1.0, base=0,
                               pattern=[[-1, 2 * H0], [0, P]], channel_multiplier=1).then_inc(consts_built, 1)
            pool.affine_select(out=head_of[:, :], in_=head_of[:, :], compare_op=ALU.is_ge, fill=0.0, base=0,
                               pattern=[[-DH, HPC]], channel_multiplier=1).then_inc(consts_built, 1)
            pool.wait_ge(consts_built, 3)
            pool.affine_select(out=head_of[:, :], in_=head_of[:, :], compare_op=ALU.is_ge, fill=0.0, base=DH - 1,
                               pattern=[[DH, HPC]], channel_multiplier=-1).then_inc(consts_built, 1)
            pool.wait_ge(weights_loaded, LOADED)

            def rstd(chain, var, result, ve, rs):
                def step(g):
                    done(pool, chain + var, g)
                    pool.tensor_tensor(rs[:, :], ve[:, :], minus_half[:, :], ALU.pow).then_inc(S[chain + result], 1)
                return step

            def C_xb(g):
                done(pool, "A_z", g)
                pool.tensor_tensor(slot(g), slot(g), beta_b[:, :], ALU.add).then_inc(S["C_xb"], 1)

            def C_hb_step(g):
                done(pool, "C_h", g)
                pool.tensor_tensor(C_hb[:, :], C_h[:, :], b2_b[:, :], ALU.add).then_inc(S["C_hb"], 1)

            def D_xb(g):
                done(pool, "D_z", g)
                pool.tensor_tensor(slot(g), slot(g), bo_b[:, :], ALU.add).then_inc(S["D_xb"], 1)

            def E_right(g):
                done(pool, "E_hc", g)
                done(pool, "E_z3", g)
                right = xs[:, g % SLOTS, F3:D]
                pool.tensor_tensor(right, right, E_h[:, 0:F3], ALU.add).then_inc(S["E_right"], 1)

            rounds(pool, POOL_ORDER, {
                "A_rstd": rstd("A", "_var", "_rstd", A_ve, A_rs), "C_xb": C_xb, "C_hb": C_hb_step,
                "C_rstd": rstd("C", "_var", "_rstd", C_ve, C_rs),
                "D_rstd": rstd("D", "_var", "_rstd", D_ve, D_rs), "D_xb": D_xb,
                "E_rstd": rstd("E", "_var", "_rstd", E_ve, E_rs),
                "E_rstd3": rstd("E", "_var3", "_rstd3", E_ve, E_rs), "E_right": E_right,
            })

        @block.scalar
        def _(act):
            for dst, src in small_loads:
                act.dma_start(dst, src).then_inc(weights_loaded, 16)
            act.wait_ge(weights_loaded, LOADED)

            def relu_copy(after, signal, dst, src):
                def step(g):
                    done(act, after, g)
                    act.activation(dst, src, ACT.Relu).then_inc(S[signal], 1)
                return step

            def copy(after, signal, dst, src):
                def step(g):
                    done(act, after, g)
                    act.activation(dst, src, ACT.Copy).then_inc(S[signal], 1)
                return step

            def A_whc_hi(g):
                done(act, "A_wh_hi", g)
                done_before(act, "B_o", g)
                act.activation(whs[:, 2:4, :].rearrange("p h d -> p (h d)"), pA[:, 1, :], ACT.Copy).then_inc(S["A_whc_hi"], 1)

            def A_whc_lo(g):
                done(act, "A_wh_lo", g)
                act.activation(whs[:, 0:2, :].rearrange("p h d -> p (h d)"), pA[:, 0, :], ACT.Copy).then_inc(S["A_whc_lo"], 1)

            def A_slope(g):
                done(act, "A_s", g)
                act.activation(A_l[:, :, :].rearrange("p h m -> p (h m)"), pA[:, 0, :], ACT.Copy, scale=SLOPE_L0)\
                   .then_inc(S["A_slope"], 1)

            def A_exp(g):
                done(act, "A_shift", g)
                flat = A_l[:, :, :].rearrange("p h m -> p (h m)")
                act.activation(flat, flat, ACT.Exp).then_inc(S["A_exp"], 1)

            def A_attn(g):
                done(act, "A_pT", g)
                done_before(act, "B_o", g)
                act.activation(attnT[:, :, :].rearrange("p h m -> p (h m)"), pA[:, 1, :], ACT.Copy).then_inc(S["A_attn"], 1)

            def B_exp(g):
                done(act, "B_o", g)
                act.activation(B_e[:, :], pB[:, :, :].rearrange("p b n -> p (b n)"), ACT.Exp).then_inc(S["B_exp"], 1)

            def B_hTc_lo(g):
                done(act, "B_hT", g)
                act.activation(B_hT[:, 0:4, :].rearrange("p k n -> p (k n)"), pB[:, 0, :], ACT.Copy).then_inc(S["B_hTc_lo"], 1)

            def B_whc(g):
                done(act, "B_wh", g)
                done_before(act, "C_o", g)
                act.activation(wh2[:, :], pB[:, 0, 0:D + 2], ACT.Copy).then_inc(S["B_whc"], 1)

            def slope(chain, dst, src, alpha):
                def step(g):
                    done(act, chain + "_s", g)
                    act.activation(dst, src, ACT.Copy, scale=alpha).then_inc(S[chain + "_slope"], 1)
                return step

            def exp_and_sum(chain, t, minus_max, total):
                def step(g):
                    done(act, chain + "_max", g)
                    act.activation(t[:, :], t[:, :], ACT.Exp, bias=minus_max[:, :], accum_out=total[:, :])\
                       .then_inc(S[chain + "_exp"], 1)
                return step

            def C_oexp(g):
                done(act, "C_o", g)
                done(act, "C_recip", g)
                act.activation(C_e[:, :], pC[:, 0:D], ACT.Exp, scale=C_rec[:, :]).then_inc(S["C_oexp"], 1)

            def C_hidc(g):
                done(act, "C_hid", g)
                act.activation(C_hid[:, 0:P], pC[:, 0:P], ACT.Relu, bias=b1_c[:, 0:1])
                act.activation(C_hid[:, P:D], pC[:, P:D], ACT.Relu, bias=b1_c[:, 1:2]).then_inc(S["C_hidc"], 1)

            def D_qc(g):
                done(act, "D_q", g)
                act.activation(D_q[:, 0, :], pD[:, 0, 0:P], ACT.Identity, bias=bq_c[:, 0:1])
                act.activation(D_q[:, 1, :], pD[:, 0, P:D], ACT.Identity, bias=bq_c[:, 1:2]).then_inc(S["D_qc"], 1)

            def D_exp(g):
                done(act, "D_shift", g)
                flat = D_s[:, :, :].rearrange("p h m -> p (h m)")
                act.activation(flat, flat, ACT.Exp, scale=SCALE).then_inc(S["D_exp"], 1)

            def E_hc(g):
                done(act, "E_h", g)
                done_before(act, "E_right", g)
                act.activation(E_h[:, :], pE[:, 0:F3 + 2], ACT.Copy).then_inc(S["E_hc"], 1)

            rounds(act, ACT_ORDER, {
                "A_hT": relu_copy("A_zT", "A_hT", A_hT[:, :], pA[:, 0, 0:D]),
                "A_whc_hi": A_whc_hi, "A_whc_lo": A_whc_lo, "A_slope": A_slope, "A_exp": A_exp, "A_attn": A_attn,
                "B_exp": B_exp, "B_hTc_lo": B_hTc_lo, "B_whc": B_whc,
                "C_slope": slope("C", C_l[:, :], pC[:, 0:P], SLOPE_L0),
                "C_exp": exp_and_sum("C", C_l, C_m, C_sum),
                "C_attn": copy("C_pT", "C_attn", C_aT[:, :], pC[:, P:2 * P]),
                "C_oexp": C_oexp,
                "C_hTc": copy("C_hT", "C_hTc", C_hT[:, :], pC[:, D:2 * D]),
                "C_hidc": C_hidc,
                "D_hT": relu_copy("D_zT", "D_hT", D_hT[:, :], pD[:, 0, 0:D]),
                "D_qc": D_qc, "D_exp": D_exp,
                "D_pTc_lo": copy("D_pT", "D_pTc_lo", D_pT[:, 0:4, :].rearrange("p h n -> p (h n)"), pD[:, 0, :]),
                "D_oTc": copy("D_oT", "D_oTc", D_oT[:, :], pD[:, 1, 0:D]),
                "E_hT": relu_copy("E_zT", "E_hT", E_hT[:, :], pE[:, 0:D]),
                "E_hT3": relu_copy("E_zT3", "E_hT3", E_hT[:, :], pE[:, D:2 * D]),
                "E_hc": E_hc,
                "E_slope": slope("E", E_l[:, :], pE[:, 384:512], SLOPE_L3),
                "E_exp": exp_and_sum("E", E_l, E_m, E_sum),
                "E_attn": copy("E_pT", "E_attn", E_aT[:, :], pE[:, 256:384]),
            })

        @block.vector
        def _(dve):
            dve.wait_ge(weights_loaded, LOADED)
            dve.wait_ge(consts_built, 4)
            dve.tensor_copy(adj_f[:, :], adj_i[:, :]).then_inc(adj_ready, 1)
            dve.wait_ge(adj_ready, 1)
            dve.tensor_reduce(deg[:, :], adj_f[:, :], AX.X, ALU.add).then_inc(dve_setup, 1)
            dve.tensor_scalar(products[:, 0:P], adj_f[:, :], 0.0, -1.0, ALU.is_gt, ALU.add).then_inc(deg_ready, 1)
            dve.wait_ge(deg_ready, 1)
            dve.tensor_scalar(mask[:, :], products[:, 0:P], -MASKED, None, ALU.mult).then_inc(dve_setup, 1)
            dve.tensor_copy(ident_bf[:, :], ident[:, :]).then_inc(dve_setup, 1)
            dve.memset(D_v[:, :, :], 1.0).then_inc(dve_setup, 1)
            dve.wait_ge(dve_setup, 4)
            count = 4
            dots = [(wh_w[:, c, h, :], a0_b[:, h, t * D:(t + 1) * D], wa_w[:, c, t * H0 + h:t * H0 + h + 1])
                    for c in range(K) for h in range(H0) for t in range(2)]
            dots += [(wout_w[:, c, 0:D], aout_b[:, t * D:(t + 1) * D], wout_w[:, c, D + t:D + t + 1])
                     for c in range(KH) for t in range(2)]
            dots += [(w3_w[:, c, 0:F3], a3_b[:, t * F3:(t + 1) * F3], w3_w[:, c, F3 + t:F3 + t + 1])
                     for c in range(K) for t in range(2)]
            for w, a, dot in dots:
                dve.tensor_tensor_reduce(products[:, 0:a.shape[1]], w, a, 1.0, 0.0, ALU.mult, ALU.add, dot)\
                   .then_inc(dve_setup, 1)
                count += 1
                dve.wait_ge(dve_setup, count)
            dve.wait_ge(adjT_done, 1)
            dve.tensor_copy(adjT[:, :], pA[:, 0, 0:P]).then_inc(dve_setup, 1)
            assert count + 1 == 5 + len(dots)

            def norm_steps(eng_x, chain, suffix, st, mv, ve, after):
                def stats(g):
                    dve.wait_ge(consts_built, 4)
                    after(g)
                    dve.bn_stats(st[:, :], eng_x(g)).then_inc(S[chain + "_stats" + suffix], 1)
                    done_apart(dve, chain + "_stats" + suffix, g)
                    dve.bn_aggr(mv[:, :], st[:, :]).then_inc(S[chain + "_moments" + suffix], 1)
                    done(dve, chain + "_moments" + suffix, g)
                    dve.tensor_scalar(ve[:, :], mv[:, 1:2], EPS, None, ALU.add).then_inc(S[chain + "_var" + suffix], 1)
                return stats

            def normalise(chain, suffix, z, mv, rs):
                def step(g):
                    done(dve, chain + "_rstd" + suffix, g)
                    dve.tensor_scalar(z[:, :], slot(g), mv[:, 0:1], rs[:, 0:1], ALU.subtract, ALU.mult)\
                       .then_inc(S[chain + "_z" + suffix], 1)
                return step

            def copy(after, signal, dst, src):
                def step(g):
                    done(dve, after, g)
                    dve.tensor_copy(dst, src).then_inc(S[signal], 1)
                return step

            def A_max(g):
                done(dve, "A_slope", g)
                flat = A_l[:, :, :].rearrange("p h m -> p (h m)")
                dve.tensor_tensor(flat, pA[:, 0, :], flat, ALU.max).then_inc(S["A_leaky"], 1)
                done(dve, "A_leaky", g)
                dve.tensor_reduce(A_m[:, :], A_l[:, :, :], AX.X, ALU.max).then_inc(S["A_max"], 1)
                done(dve, "A_max", g)
                for h in range(H0):
                    last = dve.tensor_scalar(A_l[:, h, :], A_l[:, h, :], A_m[:, h:h + 1], None, ALU.subtract)
                last.then_inc(S["A_shift"], 1)

            def A_norm(g):
                done(dve, "A_exp", g)
                dve.tensor_reduce(A_sum[:, :], A_l[:, :, :], AX.X, ALU.add).then_inc(S["A_sum"], 1)
                done(dve, "A_sum", g)
                dve.reciprocal(A_rec[:, :], A_sum[:, :]).then_inc(S["A_recip"], 1)
                done(dve, "A_recip", g)
                for h in range(H0):
                    last = dve.tensor_scalar(A_l[:, h, :], A_l[:, h, :], A_rec[:, h:h + 1], None, ALU.mult)
                last.then_inc(S["A_norm"], 1)

            def B_h(g):
                done(dve, "B_exp", g)
                dve.tensor_scalar(B_e[:, :], B_e[:, :], 1.0, -1.0, ALU.min, ALU.add).then_inc(S["B_min"], 1)
                done(dve, "B_min", g)
                dve.tensor_tensor(B_e[:, :], pB[:, :, :].rearrange("p b n -> p (b n)"), B_e[:, :], ALU.max)\
                   .then_inc(S["B_h"], 1)

            def minus_max(chain, m, t, scores):
                def step(g):
                    done(dve, chain + "_slope", g)
                    dve.tensor_tensor(t[:, :], scores, t[:, :], ALU.max).then_inc(S[chain + "_leaky"], 1)
                    done(dve, chain + "_leaky", g)
                    dve.tensor_reduce(m[:, :], t[:, :], AX.X, ALU.max, negate=True).then_inc(S[chain + "_max"], 1)
                return step

            def recip(chain, r, total):
                def step(g):
                    done(dve, chain + "_exp", g)
                    dve.reciprocal(r[:, :], total[:, :]).then_inc(S[chain + "_recip"], 1)
                return step

            def C_h_step(g):
                done(dve, "C_oexp", g)
                dve.tensor_scalar(C_e[:, :], C_e[:, :], 1.0, -1.0, ALU.min, ALU.add).then_inc(S["C_min"], 1)
                done(dve, "C_min", g)
                done_before(dve, "C_hb", g)
                dve.scalar_tensor_tensor(out=C_h[:, :], in0=pC[:, 0:D], scalar=C_rec[:, :], in1=C_e[:, :],
                                         op0=ALU.mult, op1=ALU.max).then_inc(S["C_h"], 1)

            def C_y_step(g):
                done(dve, "C_ffn", g)
                done(dve, "C_hb", g)
                dve.tensor_tensor(C_y[:, :], pC[:, D:2 * D], C_hb[:, :], ALU.add).then_inc(S["C_y"], 1)
                C_stats(g)

            def C_after_y(g):
                done(dve, "C_y", g)

            C_stats = norm_steps(lambda g: C_y[:, :], "C", "", C_st, C_mv, C_ve, C_after_y)

            def C_x1(g):
                dve.scalar_tensor_tensor(out=C_g[:, :], in0=C_y[:, :], scalar=C_mv[:, 0:1], in1=gamma_b[:, :],
                                         op0=ALU.subtract, op1=ALU.mult).then_inc(S["C_g"], 1)
                done(dve, "C_g", g)
                done(dve, "C_rstd", g)
                done(dve, "C_xb", g)
                dve.scalar_tensor_tensor(out=slot(g), in0=C_g[:, :], scalar=C_rs[:, 0:1], in1=slot(g),
                                         op0=ALU.mult, op1=ALU.add).then_inc(S["C_x1"], 1)

            def D_kc(g):
                done(dve, "D_kv", g)
                for c in range(K):
                    src = pD[:, 1, c * P:(c + 1) * P].unsqueeze(1).to_broadcast([P, HPC, P])
                    own = head_of[:, :].unsqueeze(2).to_broadcast([P, HPC, P])
                    last = dve.scalar_tensor_tensor(out=D_k[:, c, :, :], in0=src, scalar=bk_c[:, c:c + 1], in1=own,
                                                    op0=ALU.add, op1=ALU.mult)
                last.then_inc(S["D_kc"], 1)

            def D_vc(g):
                heads = lambda t: t.rearrange("p (h d) -> p h d", h=HEADS_L1)
                dve.tensor_tensor(D_v[:, :, 0:DH], heads(pD[:, 1, D:2 * D]), heads(bv_b[:, :]), ALU.add)\
                   .then_inc(S["D_vc"], 1)

            def D_max(g):
                done(dve, "D_s", g)
                s = pD[:, :, :].rearrange("p b (h n) -> p (b h) n", n=P)
                dve.tensor_reduce(D_m[:, :], s, AX.X, ALU.max).then_inc(S["D_max"], 1)
                done(dve, "D_max", g)
                dve.tensor_tensor(D_s[:, :, :], s, D_m[:, :].unsqueeze(2).to_broadcast([P, HEADS_L1, P]), ALU.subtract)\
                   .then_inc(S["D_shift"], 1)

            def D_on(g):
                done(dve, "D_o", g)
                o = pD[:, 0, 0:HEADS_L1 * (DH + 1)].rearrange("p (h d) -> p h d", h=HEADS_L1)
                dve.reciprocal(D_rec[:, :].unsqueeze(2), o[:, :, DH:DH + 1]).then_inc(S["D_recip"], 1)
                done(dve, "D_recip", g)
                dve.tensor_tensor(D_o[:, :].rearrange("p (h d) -> p h d", h=HEADS_L1), o[:, :, 0:DH],
                                  D_rec[:, :].unsqueeze(2).to_broadcast([P, HEADS_L1, DH]), ALU.mult)\
                   .then_inc(S["D_on"], 1)

            def D_x2(g):
                done(dve, "D_out", g)
                done(dve, "D_xb", g)
                dve.tensor_tensor(slot(g), pD[:, 1, D:2 * D], slot(g), ALU.add).then_inc(S["D_x2"], 1)

            def E_mj_step(g):
                done(dve, "E_m", g)
                dve.tensor_tensor(E_mj[:, :], pE[:, D:2 * D], bl2_b[:, :], ALU.add).then_inc(S["E_mj"], 1)
                dve.scalar_tensor_tensor(out=slot(g), in0=pE[:, 0:D], scalar=deg[:, :], in1=slot(g),
                                         op0=ALU.mult, op1=ALU.add).then_inc(S["E_xm"], 1)

            def E_x3(g):
                done(dve, "E_am", g)
                done(dve, "E_xm", g)
                dve.tensor_tensor(slot(g), pE[:, 0:D], slot(g), ALU.add).then_inc(S["E_x3"], 1)
                E_stats3(g)

            E_stats3 = norm_steps(slot, "E", "3", E_st, E_mv, E_ve, lambda g: done(dve, "E_x3", g))

            def E_left(g):
                done(dve, "E_o", g)
                done(dve, "E_recip", g)
                left = xs[:, g % SLOTS, 0:F3]
                dve.scalar_tensor_tensor(out=left, in0=pE[:, 384:512], scalar=E_rec[:, :], in1=left,
                                         op0=ALU.mult, op1=ALU.add).then_inc(S["E_left"], 1)

            rounds(dve, DVE_ORDER, {
                "A_stats": norm_steps(slot, "A", "", A_st, A_mv, A_ve, lambda g: dve.wait_ge(x_loaded, 16 * (g + 1))),
                "A_z": normalise("A", "", A_z, A_mv, A_rs),
                "A_fcopy": copy("A_f", "A_fcopy", A_f[:, :], pA[:, 0, 0:2 * H0]),
                "A_fTc": copy("A_fT", "A_fTc", A_fT[:, :], pA[0:2 * H0, 1, 0:P]),
                "A_max": A_max, "A_norm": A_norm,
                "B_h": B_h,
                "B_hTc_hi": copy("B_hT", "B_hTc_hi", B_hT[:, 4:8, :].rearrange("p k n -> p (k n)"), pB[:, 1, :]),
                "C_fTc": copy("C_fT", "C_fTc", C_fT[:, :], pC[0:2, 256:256 + P]),
                "C_max": minus_max("C", C_m, C_l, pC[:, 0:P]), "C_recip": recip("C", C_rec, C_sum),
                "C_h": C_h_step, "C_y": C_y_step, "C_x1": C_x1,
                "D_stats": norm_steps(slot, "D", "", D_st, D_mv, D_ve, lambda g: done(dve, "C_x1", g)),
                "D_z": normalise("D", "", D_z, D_mv, D_rs),
                "D_kc": D_kc, "D_vc": D_vc, "D_max": D_max,
                "D_pTc_hi": copy("D_pT", "D_pTc_hi", D_pT[:, 4:8, :].rearrange("p h n -> p (h n)"), pD[:, 1, :]),
                "D_on": D_on, "D_x2": D_x2,
                "E_stats": norm_steps(slot, "E", "", E_st, E_mv, E_ve, lambda g: done(dve, "D_x2", g)),
                "E_z": normalise("E", "", E_z, E_mv, E_rs),
                "E_mj": E_mj_step, "E_x3": E_x3,
                "E_z3": normalise("E", "3", E_z, E_mv, E_rs),
                "E_fTc": copy("E_fT", "E_fTc", E_fT[:, :], pE[0:2, 256:384]),
                "E_max": minus_max("E", E_m, E_l, pE[:, 384:512]), "E_recip": recip("E", E_rec, E_sum),
                "E_left": E_left,
            })

        @block.tensor
        def _(pe):
            pe.wait_ge(consts_built, 4)
            pe.wait_ge(adj_ready, 1)
            pe.transpose(pA[:, 0, 0:P], adj_f[:, :], ident[:, :]).then_inc(adjT_done, 1)
            pe.wait_ge(weights_loaded, LOADED)
            pe.wait_ge(dve_setup, 5 + len([0] * (2 * K * H0 + 2 * KH + 2 * K)))

            def transposes(dst, src, n):
                for j in range(n):
                    last = pe.transpose(dst[:, j * P:(j + 1) * P], src[:, j * P:(j + 1) * P], ident[:, :])
                return last

            def add_mask(dst, heads):
                m = mask[:, :] if heads == 1 else mask[:, :].unsqueeze(1).to_broadcast([P, heads, P])
                pe.matmul(dst, ident_bf[:, :], m, start=True, stop=False)

            def project(dst, hT, w):
                for k in range(K):
                    last = pe.matmul(dst, hT[:, k * P:(k + 1) * P], w[:, k, :], start=(k == 0), stop=(k == K - 1))
                return last

            def A_zT(g):
                done(pe, "A_z", g)
                done_before(pe, "A_attn", g)
                transposes(pA[:, 0, :], A_z, K).then_inc(S["A_zT"], 1)

            def A_wh(g):
                done(pe, "A_hT", g)
                project(pA[:, 0, 0:2 * H0], A_hT, wa_w).then_inc(S["A_f"], 1)
                project(pA[:, 1, :], A_hT, wh_w[:, :, 2:4, :].rearrange("p k h d -> p k (h d)")).then_inc(S["A_wh_hi"], 1)
                done(pe, "A_fcopy", g)
                project(pA[:, 0, :], A_hT, wh_w[:, :, 0:2, :].rearrange("p k h d -> p k (h d)")).then_inc(S["A_wh_lo"], 1)

            def A_fT_step(g):
                done(pe, "A_whc_hi", g)
                pe.transpose(pA[0:2 * H0, 1, 0:P], A_f[:, :], ident[:, :]).then_inc(S["A_fT"], 1)

            def A_s(g):
                done(pe, "A_fTc", g)
                done(pe, "A_whc_lo", g)
                add_mask(pA[:, 0, :].rearrange("p (h m) -> p h m", h=H0), H0)
                pe.matmul(pA[:, 0, :], A_fT[:, :], rows[:, 0:H0, :].rearrange("r h m -> r (h m)"), start=False, stop=False)
                for h in range(H0):
                    last = pe.matmul(pA[:, 0, h * P:(h + 1) * P], rows[:, H0 + h, :], A_fT[:, :],
                                     start=False, stop=(h == H0 - 1))
                last.then_inc(S["A_s"], 1)

            def A_pT(g):
                done(pe, "A_norm", g)
                transposes(pA[:, 1, :], A_l[:, :, :].rearrange("p h m -> p (h m)"), H0).then_inc(S["A_pT"], 1)

            def B_o(g):
                done(pe, "A_attn", g)
                done_before(pe, "B_whc", g)
                for h in range(H0):
                    last = pe.matmul(pB[:, h // 2, (h % 2) * D:(h % 2 + 1) * D], attnT[:, h, :], whs[:, h, :],
                                     start=True, stop=True)
                last.then_inc(S["B_o"], 1)

            def B_hT_step(g):
                done(pe, "B_h", g)
                transposes(pB[:, :, :].rearrange("p b n -> p (b n)"), B_e, KH).then_inc(S["B_hT"], 1)

            def B_wh(g):
                done(pe, "B_hTc_lo", g)
                for k in range(KH):
                    if k == KH // 2:
                        done(pe, "B_hTc_hi", g)
                    last = pe.matmul(pB[:, 0, 0:D + 2], B_hT[:, k, :], wout_w[:, k, :], start=(k == 0), stop=(k == KH - 1))
                last.then_inc(S["B_wh"], 1)

            def C_fT_step(g):
                done(pe, "B_whc", g)
                done_before(pe, "C_y", g)
                pe.transpose(pC[0:2, 256:256 + P], wh2[:, D:D + 2], ident[:, :]).then_inc(S["C_fT"], 1)

            def one_head(dst, fT, signal):
                add_mask(dst, 1)
                pe.matmul(dst, fT[:, :], rows[0:2, 0, :], start=False, stop=False)
                pe.matmul(dst, rows[0:2, 1, :], fT[:, :], start=False, stop=True).then_inc(S[signal], 1)

            def C_s(g):
                done(pe, "C_fTc", g)
                one_head(pC[:, 0:P], C_fT, "C_s")

            def C_pT(g):
                done(pe, "C_exp", g)
                pe.transpose(pC[:, P:2 * P], C_l[:, :], ident[:, :]).then_inc(S["C_pT"], 1)

            def C_o(g):
                done(pe, "C_attn", g)
                pe.matmul(pC[:, 0:D], C_aT[:, :], wh2[:, 0:D], start=True, stop=True).then_inc(S["C_o"], 1)

            def C_hT_step(g):
                done(pe, "C_h", g)
                transposes(pC[:, D:2 * D], C_h, K).then_inc(S["C_hT"], 1)

            def transposed_product(dst, w, hT):
                for c in range(K):
                    for k in range(K):
                        last = pe.matmul(dst[:, c * P:(c + 1) * P], w[:, k, c * P:(c + 1) * P], hT[:, k * P:(k + 1) * P],
                                         start=(k == 0), stop=(k == K - 1))
                return last

            def C_hid_step(g):
                done(pe, "C_hTc", g)
                transposed_product(pC[:, 0:D], w1_w, C_hT).then_inc(S["C_hid"], 1)

            def C_ffn(g):
                done(pe, "C_hidc", g)
                project(pC[:, D:2 * D], C_hid, w2_w).then_inc(S["C_ffn"], 1)

            def D_zT(g):
                done(pe, "D_z", g)
                done_before(pe, "D_x2", g)
                transposes(pD[:, 0, :], D_z, K).then_inc(S["D_zT"], 1)

            def D_qkv(g):
                done(pe, "D_hT", g)
                transposed_product(pD[:, 0, 0:D], wq_w, D_hT).then_inc(S["D_q"], 1)
                transposed_product(pD[:, 1, 0:D], wk_w, D_hT)
                project(pD[:, 1, D:2 * D], D_hT, wv_w).then_inc(S["D_kv"], 1)

            def D_s_step(g):
                done(pe, "D_qc", g)
                done(pe, "D_kc", g)
                done(pe, "D_vc", g)
                for c in range(K):
                    add_mask(pD[:, c, :].rearrange("p (h m) -> p h m", h=HPC), HPC)
                    last = pe.matmul(pD[:, c, :], D_q[:, c, :], D_k[:, c, :, :].rearrange("p h m -> p (h m)"),
                                     start=False, stop=True)
                last.then_inc(S["D_s"], 1)

            def D_pT_step(g):
                done(pe, "D_exp", g)
                transposes(pD[:, :, :].rearrange("p b n -> p (b n)"), D_s[:, :, :].rearrange("p h m -> p (h m)"), HEADS_L1)\
                    .then_inc(S["D_pT"], 1)

            def D_o_step(g):
                done(pe, "D_pTc_lo", g)
                for h in range(HEADS_L1):
                    if h == HPC:
                        done(pe, "D_pTc_hi", g)
                    last = pe.matmul(pD[:, 0, h * (DH + 1):(h + 1) * (DH + 1)], D_pT[:, h, :], D_v[:, h, :],
                                     start=True, stop=True)
                last.then_inc(S["D_o"], 1)

            def D_oT_step(g):
                done(pe, "D_on", g)
                transposes(pD[:, 1, :], D_o, K).then_inc(S["D_oT"], 1)

            def D_out(g):
                done(pe, "D_oTc", g)
                project(pD[:, 1, D:2 * D], D_oT, wo_w).then_inc(S["D_out"], 1)

            def E_zT(g):
                done(pe, "E_z", g)
                done_before(pe, "E_left", g)
                transposes(pE[:, 0:D], E_z, K).then_inc(S["E_zT"], 1)

            def E_m(g):
                done(pe, "E_hT", g)
                project(pE[:, :], E_hT, wij_w).then_inc(S["E_m"], 1)

            def E_am(g):
                done(pe, "E_mj", g)
                done(pe, "E_xm", g)
                pe.matmul(pE[:, 0:D], adjT[:, :], E_mj[:, :], start=True, stop=True).then_inc(S["E_am"], 1)

            def E_zT3(g):
                done(pe, "E_z3", g)
                transposes(pE[:, D:2 * D], E_z, K).then_inc(S["E_zT3"], 1)

            def E_h_step(g):
                done(pe, "E_hT3", g)
                project(pE[:, 0:F3 + 2], E_hT, w3_w).then_inc(S["E_h"], 1)

            def E_fT_step(g):
                done(pe, "E_hc", g)
                pe.transpose(pE[0:2, 256:384], E_h[:, F3:F3 + 2], ident[:, :]).then_inc(S["E_fT"], 1)

            def E_s(g):
                done(pe, "E_fTc", g)
                one_head(pE[:, 384:512], E_fT, "E_s")

            def E_pT(g):
                done(pe, "E_exp", g)
                pe.transpose(pE[:, 256:384], E_l[:, :], ident[:, :]).then_inc(S["E_pT"], 1)

            def E_o(g):
                done(pe, "E_attn", g)
                pe.matmul(pE[:, 384:512], E_aT[:, :], E_h[:, 0:F3], start=True, stop=True).then_inc(S["E_o"], 1)

            rounds(pe, PE_ORDER, {
                "A_zT": A_zT, "A_wh": A_wh, "A_fT": A_fT_step, "A_s": A_s, "A_pT": A_pT,
                "B_o": B_o, "B_hT": B_hT_step, "B_wh": B_wh,
                "C_fT": C_fT_step, "C_s": C_s, "C_pT": C_pT, "C_o": C_o, "C_hT": C_hT_step, "C_hid": C_hid_step,
                "C_ffn": C_ffn,
                "D_zT": D_zT, "D_qkv": D_qkv, "D_s": D_s_step, "D_pT": D_pT_step, "D_o": D_o_step, "D_oT": D_oT_step,
                "D_out": D_out,
                "E_zT": E_zT, "E_m": E_m, "E_am": E_am, "E_zT3": E_zT3, "E_h": E_h_step, "E_fT": E_fT_step, "E_s": E_s,
                "E_pT": E_pT, "E_o": E_o,
            })


def kernel(**inputs):
    import numpy as np
    import concourse.bacc as bacc
    from concourse import mybir as mb
    from concourse.bass_utils import run_bass_kernel_spmd as run

    def transposed(a):
        return np.ascontiguousarray(np.asarray(a).T)

    def columns(a):
        return transposed(np.asarray(a).reshape(-1, 128))

    plain = lambda name: np.ascontiguousarray(np.asarray(inputs[name]))
    w_l2 = plain("L2_gnn_W")
    d = w_l2.shape[0]
    arrays = {
        "x": plain("x"), "adj": plain("adj"),
        "w_heads": plain("L0_gnn_W_heads"), "a_heads": plain("L0_gnn_a_heads"),
        "w_out": plain("L0_gnn_W_out"), "a_out": plain("L0_gnn_a_out"),
        "w1": plain("L0_gnn_w1"), "b1": columns(inputs["L0_gnn_b1"]), "w2": plain("L0_gnn_w2"), "b2": plain("L0_gnn_b2"),
        "gamma": plain("L0_gnn_ln_gamma"), "beta": plain("L0_gnn_ln_beta"),
        "wqT": transposed(inputs["L1_gnn_Wq"]), "bq": columns(inputs["L1_gnn_bq"]),
        "wkT": transposed(inputs["L1_gnn_Wk"]), "bk": columns(inputs["L1_gnn_bk"]),
        "wvT": transposed(inputs["L1_gnn_Wv"]), "bv": plain("L1_gnn_bv"),
        "woT": transposed(inputs["L1_gnn_Wo"]), "bo": plain("L1_gnn_bo"),
        "wijT": np.ascontiguousarray(np.concatenate([w_l2[:, :d].T, w_l2[:, d:].T], axis=1)),
        "b_l2": plain("L2_gnn_b"),
        "w_l3": plain("L3_gnn_W"), "a_l3": plain("L3_gnn_a"),
    }
    nc = bacc.Bacc("TRN2", target_bir_lowering=False, num_devices=1)
    args = [nc.dram_tensor(f"in_{n}", a.shape, mb.dt.from_np(a.dtype), kind="ExternalInput").ap()
            for n, a in arrays.items()]
    out = nc.dram_tensor("out_x", arrays["x"].shape, mb.dt.float32, kind="ExternalOutput").ap()
    gnn_stack(nc, *args, out)
    r = run(nc, [{f"in_{n}": a for n, a in arrays.items()}], core_ids=[0])
    return r.results[0]["out_x"]
```

```python
import concourse.bass as bass
from concourse import mybir
from contextlib import ExitStack

ALU = mybir.AluOpType
ACT = mybir.ActivationFunctionType
AX = mybir.AxisListType
F32 = mybir.dt.float32
BF16 = mybir.dt.bfloat16
F32R = mybir.dt.float32r
I32 = mybir.dt.int32

EPS = 1e-5
MASKED = -1e11
SLOPE_L0 = 0.01
SLOPE_L3 = 0.2
HEADS_L1 = 8
SLOTS = 8

CHAINS = "ABCDFE"

PE_ORDER = """
B_o F_s.0 C_fT A_zT F_s C_s A_f E_ah A_wh_hi A_wh_lo E_m C_pT D_zT A_fT F_pT C_o D_k.0 A_s E_zT3 D_kv C_hT E_h
F_o.0 C_hid B_wh.0 E_fT F_o B_wh.1 E_s C_ffn B_wh.2 F_oT D_q A_pT E_pT B_wh E_o F_out
""".split()
ACT_ORDER = """
B_exp A_hT E_high A_high C_slope A_fc E_ahhigh F_exp A_whc_hi C_exp B_high D_hT C_attn D_high A_whc_lo C_oexp
F_pTc E_hT3 A_slope D_kc C_hTc E_hc C_hidc C_high A_exp E_slope F_high E_exp D_qc E_attn A_attn B_whc D_qhigh
""".split()
DVE_ORDER = """
A_stats E_stats A_moments D_stats A_z E_moments E_z D_moments C_fTc E_low F_max E_ahlow B_h C_leaky C_max D_z
C_recip E_x3 A_fTc E_stats3 E_moments3 B_low E_z3 C_min C_h A_leaky A_max D_khigh D_klow E_fTc F_recip F_on
D_vc A_recip A_norm E_leaky E_max C_y E_recip C_stats C_moments F_low C_g C_x1 E_left F_x2
""".split()
POOL_ORDER = """
C_fcopy A_rstd E_rstd A_low A_fcopy E_xb C_xb D_rstd D_xb B_low2 E_rstd3 D_low E_fcopy E_right C_low C_hb
C_rstd D_qlow
""".split()

STEP_SEMAPHORES = """
A_stats A_moments A_var A_rstd A_z A_zT A_hT A_high A_low A_f A_fc A_fhi A_frest A_fmid A_fcopy A_wh_hi A_wh_lo A_whc_hi A_whc_lo A_fT A_fTc A_s A_slope A_leaky
A_max A_exp A_recip A_norm A_pT A_attn
B_o B_neg B_exp B_h B_high B_low B_low2 B_wh B_whc
C_fhi C_frest C_fmid C_fcopy C_fT C_fTc C_s C_slope C_leaky C_max C_exp C_recip C_pT C_attn C_o C_oexp C_min C_h C_hb C_hT C_hTc C_hid C_hidc C_high C_low C_ffn C_y
C_stats C_moments C_var C_rstd C_xb C_g C_x1
D_stats D_moments D_var D_rstd D_z D_xb D_zT D_hT D_high D_low D_kv D_kc D_khigh D_klow D_vc D_q D_qc D_qhigh D_qlow 
F_s F_max F_exp F_pT F_pTc
F_o F_recip F_on F_oT F_high F_low F_out F_x2
E_stats E_moments E_var E_rstd E_z E_high E_low E_xb E_ah E_ahhigh E_ahlow E_m E_x3
E_stats3 E_moments3 E_var3 E_rstd3 E_z3 E_zT3 E_hT3 E_h E_hc E_fhi E_frest E_fmid E_fcopy E_fT E_fTc E_s E_slope E_leaky E_max E_exp E_recip E_pT E_attn
E_o E_left E_right
""".split()


def gnn_stack(nc, x, adj, w_heads, a_heads, w_out, a_out, w1, b1, w2, b2, gamma, beta,
              wqT, bq, wkT, bk, wvT, bv, woT, bo, wijT, b_l2, w_l3, a_l3, out):
    GRAPHS, N, D = x.shape
    P = 128
    assert N == P and D == 2 * P
    K = D // P
    H0 = w_heads.shape[0]
    HD = H0 * D
    KH = HD // P
    DH = D // HEADS_L1
    HPC = P // DH
    F3 = w_l3.shape[1]
    SCALE = float(DH) ** -0.5

    with ExitStack() as ctx:
        def sb(name, shape, dt=F32):
            return ctx.enter_context(nc.sbuf_tensor(name, shape, dt))

        def ps(name, shape):
            return ctx.enter_context(nc.psum_tensor(name, shape, F32))

        def sem(name):
            return ctx.enter_context(nc.semaphore(name))

        ident = sb("ident", [P, P])
        ident_bf = sb("ident_bf", [P, P], BF16)
        pick0 = sb("pick0", [P, 2 * H0, P], BF16)
        pick = sb("pick", [P, 2, P], BF16)
        adj_i = sb("adj_i", [P, P], I32)
        adj_f = sb("adj_f", [P, P])
        adj_deg = sb("adj_deg", [P, 2 * P], F32R)
        mask = sb("mask", [P, P], BF16)
        deg = sb("deg", [P, 1])
        minus_half = sb("minus_half", [P, 1])
        eps = sb("eps", [P, 1])
        zeros = sb("zeros", [P, 2 * H0])
        wh_w = sb("wh_w", [P, K, H0, D])
        wa_w = sb("wa_w", [P, K, P])
        a0_b = sb("a0_b", [P, H0, 2 * D])
        wout_w = sb("wout_w", [P, KH, D + 2])
        aout_b = sb("aout_b", [P, 2 * D])
        w1_w = sb("w1_w", [P, K, D])
        w2_w = sb("w2_w", [P, K, D])
        b1_c = sb("b1_c", [P, K])
        b2_b = sb("b2_b", [P, D])
        gamma_b = sb("gamma_b", [P, D])
        beta_b = sb("beta_b", [P, D])
        wq_w = sb("wq_w", [P, K, D])
        wk_w = sb("wk_w", [P, K, D])
        wv_w = sb("wv_w", [P, K, D])
        wo_w = sb("wo_w", [P, K, D])
        bq_c = sb("bq_c", [P, K])
        bk_c = sb("bk_c", [P, K])
        bv_b = sb("bv_b", [P, D])
        bo_b = sb("bo_b", [P, D])
        wij_w = sb("wij_w", [P, K, 2 * D])
        bl2_b = sb("bl2_b", [P, D])
        w3_w = sb("w3_w", [P, K, F3 + 2])
        a3_b = sb("a3_b", [P, 2 * F3])
        deg_bl2 = sb("deg_bl2", [P, D])
        products = sb("products", [P, D])

        def high_low(name, shape):
            return sb(name + "_high", shape, F32R), sb(name + "_low", shape, F32R)

        wh_hl = high_low("wh", [P, K, H0, D])
        wout_hl = high_low("wout", [P, KH, D + 2])
        w2_hl = high_low("w2", [P, K, D])
        wv_hl = high_low("wv", [P, K, D])
        wo_hl = high_low("wo", [P, K, D])
        wij_hl = high_low("wij", [P, K, 2 * D])

        xs = sb("xs", [P, SLOTS, D])

        A_st, A_mv, A_ve, A_rs = sb("A_st", [P, 6]), sb("A_mv", [P, 2]), sb("A_ve", [P, 1]), sb("A_rs", [P, 1])
        A_z, A_hT = sb("A_z_t", [P, D]), sb("A_hT_t", [P, D])
        A_hl = high_low("A_hT", [P, D])
        A_f = sb("A_f_t", [P, 2 * H0])
        A_f3, A_frest = sb("A_f3", [P, 3 * 2 * H0], BF16), sb("A_frest_t", [P, 2 * H0])
        A_fT = sb("A_fT_t", [P, P], BF16)
        A_l = sb("A_l", [P, H0, P])
        A_m, A_sum, A_rec = sb("A_m", [P, H0]), sb("A_sum_t", [P, H0]), sb("A_rec", [P, H0])
        whs = sb("whs", [P, H0, D])
        attnT = sb("attnT", [P, H0, P])
        B_e = sb("B_e", [P, HD])
        B_hl = high_low("B_h", [P, HD])
        wh2 = sb("wh2", [P, D + 2])
        C_f3, C_frest, C_fT = sb("C_f3", [P, 3 * 2], BF16), sb("C_frest_t", [P, 2]), sb("C_fT_t", [P, P], BF16)
        C_l, C_aT = sb("C_l", [P, P]), sb("C_aT", [P, P])
        C_m, C_sum, C_rec = sb("C_m", [P, 1]), sb("C_sum", [P, 1]), sb("C_rec", [P, 1])
        C_e, C_h, C_hb, C_hT, C_hid = (sb(n, [P, D]) for n in ("C_e", "C_h_t", "C_hb_t", "C_hT_t", "C_hid_t"))
        C_hl = high_low("C_hid", [P, D])
        C_y, C_g = sb("C_y_t", [P, D]), sb("C_g_t", [P, D])
        C_st, C_mv, C_ve, C_rs = sb("C_st", [P, 6]), sb("C_mv", [P, 2]), sb("C_ve", [P, 1]), sb("C_rs", [P, 1])
        D_st, D_mv, D_ve, D_rs = sb("D_st", [P, 6]), sb("D_mv", [P, 2]), sb("D_ve", [P, 1]), sb("D_rs", [P, 1])
        D_z, D_hT = sb("D_z_t", [P, D]), sb("D_hT_t", [P, D])
        D_hl = high_low("D_hT", [P, D])
        D_q, D_k = sb("D_q_t", [P, D]), sb("D_k_t", [P, K, P])
        D_qhl = high_low("D_q", [P, D])
        D_khl = high_low("D_k", [P, K, HPC, P])
        D_v = sb("D_v_t", [P, HEADS_L1 + P // (DH + 1), DH + 1])
        F_s = sb("F_s_t", [P, HEADS_L1, P])
        F_pT = sb("F_pT_t", [P, HEADS_L1, P])
        F_m, F_rec = sb("F_m", [P, HEADS_L1]), sb("F_rec", [P, HEADS_L1])
        F_o = sb("F_o_t", [P, D])
        F_hl = high_low("F_oT", [P, D])
        E_st, E_mv, E_ve, E_rs = sb("E_st", [P, 6]), sb("E_mv", [P, 2]), sb("E_ve", [P, 1]), sb("E_rs", [P, 1])
        E_z, E_hT = sb("E_z_t", [P, D]), sb("E_hT_t", [P, D])
        E_hl = high_low("E_h", [P, D])
        E_ahl = high_low("E_ah", [P, 2 * D])
        E_h = sb("E_h_t", [P, F3 + 2])
        E_f3, E_frest, E_fT = sb("E_f3", [P, 3 * 2], BF16), sb("E_frest_t", [P, 2]), sb("E_fT_t", [P, P], BF16)
        E_l, E_aT = sb("E_l", [P, P]), sb("E_aT", [P, P])
        E_m, E_sum, E_rec = sb("E_m_t", [P, 1]), sb("E_sum", [P, 1]), sb("E_rec", [P, 1])

        pA = ps("pA", [P, 2, 512])
        pB = ps("pB", [P, 2, 512])
        pC = ps("pC", [P, 512])
        pF = ps("pF", [P, 2, 512])
        pE = ps("pE", [P, 512])

        S = {name: sem(name) for name in STEP_SEMAPHORES}
        weights_loaded = sem("weights_loaded")
        zeroed = sem("zeroed")
        consts_built = sem("consts_built")
        adj_ready = sem("adj_ready")
        adjT_done = sem("adjT_done")
        deg_ready = sem("deg_ready")
        dve_setup = sem("dve_setup")
        bq_scaled = sem("bq_scaled")
        x_loaded = sem("x_loaded")
        stored = sem("stored")

        def slot(g):
            return xs[:, g % SLOTS, :]

        def done(eng, name, g):
            eng.wait_ge(S[name], g + 1)

        def done_apart(eng, name, g):
            eng.wait_ge(consts_built, BUILT)
            done(eng, name, g)

        def done_before(eng, name, g):
            if not (isinstance(g, int) and g == 0):
                eng.wait_ge(S[name], g)

        def done_in_round(eng, name, chain, g, back=0):
            other = g + CHAINS.index(chain) - CHAINS.index(name[0]) - back
            if not isinstance(other, int) or 0 <= other < GRAPHS:
                done(eng, name, other)

        def rounds(eng, order, steps):
            def one(i):
                for name in order:
                    g = i - CHAINS.index(name[0])
                    if not isinstance(g, int) or 0 <= g < GRAPHS:
                        steps[name](g)
            for i in range(len(CHAINS)):
                one(i)
            with eng.Fori(len(CHAINS), GRAPHS) as i:
                one(i)
            for i in range(GRAPHS, GRAPHS + len(CHAINS) - 1):
                one(i)

        small_loads = [
            (b1_c[:, :], b1),
            (bq_c[:, :], bq),
            (bk_c[:, :], bk),
            (b2_b[:, :], b2.partition_broadcast(P)),
            (gamma_b[:, :], gamma.partition_broadcast(P)),
            (beta_b[:, :], beta.partition_broadcast(P)),
            (bv_b[:, :], bv.partition_broadcast(P)),
            (bo_b[:, :], bo.partition_broadcast(P)),
            (bl2_b[:, :], b_l2.partition_broadcast(P)),
            (aout_b[:, :], a_out.partition_broadcast(P)),
            (a3_b[:, :], a_l3.rearrange("t f one -> (t f one)").partition_broadcast(P)),
            (a0_b[:, :, :].rearrange("p h d -> p (h d)"), a_heads.rearrange("h d -> (h d)").partition_broadcast(P)),
        ]
        loads = [(adj_i[:, :], adj)]
        loads += [(wh_w[:, c, :, :], w_heads[:, c * P:(c + 1) * P, :].rearrange("h p d -> p h d")) for c in range(K)]
        loads += [(wout_w[:, :, 0:D], w_out.rearrange("(k p) d -> p k d", p=P)),
                  (w3_w[:, :, 0:F3], w_l3.rearrange("(k p) d -> p k d", p=P))]
        loads += [(t[:, :, :], w.rearrange("(k p) d -> p k d", p=P))
                  for t, w in ((w1_w, w1), (w2_w, w2), (wq_w, wqT), (wk_w, wkT), (wv_w, wvT), (wo_w, woT), (wij_w, wijT))]
        ZEROED, BUILT = 13, 7
        DVE_SETUP = 6 + 2 * (K * H0 + KH + K) + 2 * 6
        LOADED = 16 * (len(loads) + len(small_loads))

        block = ctx.enter_context(nc.Block())

        @block.sync
        def _(sp):
            for dst, src in loads:
                sp.dma_start(dst, src).then_inc(weights_loaded, 16)

            def load(g, freed):
                if freed:
                    sp.wait_ge(stored, 16 * (g - SLOTS + 1))
                if not (isinstance(g, int) and g == 0):
                    sp.wait_ge(x_loaded, 16 * g)
                sp.dma_start(slot(g), x[g]).then_inc(x_loaded, 16)

            def store(g):
                done(sp, "E_left", g)
                done(sp, "E_right", g)
                sp.dma_start(out[g], slot(g)).then_inc(stored, 16)

            for g in range(SLOTS):
                load(g, freed=False)
            with sp.Fori(0, GRAPHS - SLOTS) as g:
                store(g)
                load(g + SLOTS, freed=True)
            for g in range(GRAPHS - SLOTS, GRAPHS):
                sp.wait_ge(stored, 16 * g)
                store(g)
            sp.wait_ge(stored, 16 * GRAPHS)

        @block.gpsimd
        def _(pool):
            pool.memset(ident[:, :], 0.0).then_inc(zeroed, 1)
            pool.memset(pick0[:, :, :], 0.0).then_inc(zeroed, 1)
            pool.memset(pick[:, :, :], 0.0).then_inc(zeroed, 1)
            for t in D_khl:
                pool.memset(t[:, :, :, :].bitcast(F32), 0.0).then_inc(zeroed, 1)
            pool.memset(minus_half[:, :], -0.5).then_inc(zeroed, 1)
            pool.memset(eps[:, :], EPS).then_inc(zeroed, 1)
            pool.memset(zeros[:, :], 0.0).then_inc(zeroed, 1)
            for t in (A_fT, C_fT, E_fT):
                pool.memset(t[:, :], 0.0).then_inc(zeroed, 1)
            pool.memset(wa_w[:, :, :], 0.0).then_inc(zeroed, 1)
            pool.memset(D_v[:, :, :], 1.0).then_inc(zeroed, 1)
            pool.wait_ge(zeroed, ZEROED)
            pool.affine_select(out=ident[:, :], in_=ident[:, :], compare_op=ALU.not_equal, fill=1.0, base=0,
                               pattern=[[-1, P]], channel_multiplier=1).then_inc(consts_built, 1)
            built = 1
            for t, logits in ((pick0, 2 * H0), (pick, 2)):
                for part in range(3):
                    pool.affine_select(out=t[:, :, :], in_=t[:, :, :], compare_op=ALU.not_equal, fill=1.0,
                                       base=-part * logits, pattern=[[-1, logits], [0, P]], channel_multiplier=1)\
                        .then_inc(consts_built, 1)
                    built += 1
                    pool.wait_ge(consts_built, built)
            assert built == BUILT
            pool.wait_ge(weights_loaded, LOADED)

            def rstd(chain, suffix, mv, ve, rs):
                def step(g):
                    done(pool, chain + "_moments" + suffix, g)
                    pool.tensor_tensor(ve[:, :], mv[:, 1:2], eps[:, :], ALU.add).then_inc(S[chain + "_var" + suffix], 1)
                    done(pool, chain + "_var" + suffix, g)
                    pool.tensor_tensor(rs[:, :], ve[:, :], minus_half[:, :], ALU.pow)\
                        .then_inc(S[chain + "_rstd" + suffix], 1)
                return step

            def split_in_three(chain, after, f, f3, rest):
                n = f.shape[1]
                signal = lambda name: S[chain + name]
                zero = zeros[:, 0:n]

                def step(g):
                    done(pool, after, g)
                    pool.tensor_tensor(f3[:, 0:n], f, zero, ALU.add).then_inc(signal("_fhi"), 1)
                    done(pool, chain + "_fhi", g)
                    pool.tensor_tensor(rest[:, :], f, f3[:, 0:n], ALU.subtract).then_inc(signal("_frest"), 1)
                    done(pool, chain + "_frest", g)
                    pool.tensor_tensor(f3[:, n:2 * n], rest[:, :], zero, ALU.add).then_inc(signal("_fmid"), 1)
                    done(pool, chain + "_fmid", g)
                    pool.tensor_tensor(f3[:, 2 * n:3 * n], rest[:, :], f3[:, n:2 * n], ALU.subtract)\
                        .then_inc(signal("_fcopy"), 1)
                return step

            def low_part(after, signal, hl, x, cols):
                def step(g):
                    done(pool, after, g)
                    pool.tensor_tensor(hl[1][:, cols], x[:, cols], hl[0][:, cols].bitcast(F32), ALU.subtract)\
                        .then_inc(S[signal], 1)
                return step

            def C_xb(g):
                done(pool, "A_z", g)
                pool.tensor_tensor(slot(g), slot(g), beta_b[:, :], ALU.add).then_inc(S["C_xb"], 1)

            def C_hb_step(g):
                done(pool, "C_h", g)
                pool.tensor_tensor(C_hb[:, :], C_h[:, :], b2_b[:, :], ALU.add).then_inc(S["C_hb"], 1)

            def D_xb(g):
                done(pool, "D_z", g)
                pool.tensor_tensor(slot(g), slot(g), bo_b[:, :], ALU.add).then_inc(S["D_xb"], 1)

            def E_xb(g):
                done(pool, "E_z", g)
                pool.tensor_tensor(slot(g), slot(g), deg_bl2[:, :], ALU.add).then_inc(S["E_xb"], 1)

            def E_right(g):
                done(pool, "E_hc", g)
                done(pool, "E_z3", g)
                right = xs[:, g % SLOTS, F3:D]
                pool.tensor_tensor(right, right, E_h[:, 0:F3], ALU.add).then_inc(S["E_right"], 1)

            rounds(pool, POOL_ORDER, {
                "A_rstd": rstd("A", "", A_mv, A_ve, A_rs), "C_rstd": rstd("C", "", C_mv, C_ve, C_rs),
                "D_rstd": rstd("D", "", D_mv, D_ve, D_rs), "E_rstd": rstd("E", "", E_mv, E_ve, E_rs),
                "E_rstd3": rstd("E", "3", E_mv, E_ve, E_rs),
                "A_fcopy": split_in_three("A", "A_fc", A_f[:, :], A_f3, A_frest),
                "C_fcopy": split_in_three("C", "B_whc", wh2[:, D:D + 2], C_f3, C_frest),
                "E_fcopy": split_in_three("E", "E_hc", E_h[:, F3:F3 + 2], E_f3, E_frest),
                "A_low": low_part("A_high", "A_low", A_hl, A_hT, slice(0, D)),
                "B_low2": low_part("B_high", "B_low2", B_hl, B_e, slice(HD // 2, HD)),
                "C_low": low_part("C_high", "C_low", C_hl, C_hid, slice(0, D)),
                "D_low": low_part("D_high", "D_low", D_hl, D_hT, slice(0, D)),
                "D_qlow": low_part("D_qhigh", "D_qlow", D_qhl, D_q, slice(0, D)),
                "C_xb": C_xb, "C_hb": C_hb_step, "D_xb": D_xb, "E_xb": E_xb, "E_right": E_right,
            })

        @block.scalar
        def _(act):
            for dst, src in small_loads:
                act.dma_start(dst, src).then_inc(weights_loaded, 16)
            act.wait_ge(weights_loaded, LOADED)
            act.wait_ge(bq_scaled, 1)

            def relu_copy(after, signal, dst, src):
                def step(g):
                    done(act, after, g)
                    act.activation(dst, src, ACT.Relu).then_inc(S[signal], 1)
                return step

            def copy(after, signal, dst, src):
                def step(g):
                    done(act, after, g)
                    act.activation(dst, src, ACT.Copy).then_inc(S[signal], 1)
                return step

            def A_whc_hi(g):
                done(act, "A_wh_hi", g)
                done_before(act, "B_o", g)
                act.activation(whs[:, 2:4, :].rearrange("p h d -> p (h d)"), pA[:, 1, :], ACT.Copy).then_inc(S["A_whc_hi"], 1)

            def A_whc_lo(g):
                done(act, "A_wh_lo", g)
                act.activation(whs[:, 0:2, :].rearrange("p h d -> p (h d)"), pA[:, 0, :], ACT.Copy).then_inc(S["A_whc_lo"], 1)

            def A_slope(g):
                done(act, "A_s", g)
                act.activation(A_l[:, :, :].rearrange("p h m -> p (h m)"), pA[:, 0, :], ACT.Copy, scale=SLOPE_L0)\
                   .then_inc(S["A_slope"], 1)

            def A_exp(g):
                done(act, "A_max", g)
                for h in range(H0):
                    last = act.activation(A_l[:, h, :], A_l[:, h, :], ACT.Exp, bias=A_m[:, h:h + 1],
                                          accum_out=A_sum[:, h:h + 1])
                last.then_inc(S["A_exp"], 1)

            def A_attn(g):
                done(act, "A_pT", g)
                done_before(act, "B_o", g)
                act.activation(attnT[:, :, :].rearrange("p h m -> p (h m)"), pA[:, 1, :], ACT.Copy).then_inc(S["A_attn"], 1)

            def B_exp(g):
                done(act, "B_o", g)
                act.activation(B_e[:, :], pB[:, :, :].rearrange("p b n -> p (b n)"), ACT.Relu, scale=-1.0)\
                   .then_inc(S["B_neg"], 1)
                done(act, "B_neg", g)
                act.activation(B_e[:, :], B_e[:, :], ACT.Exp, scale=-1.0).then_inc(S["B_exp"], 1)

            def B_whc(g):
                done(act, "B_wh", g)
                done_before(act, "C_o", g)
                act.activation(wh2[:, :], pB[:, 0, 0:D + 2], ACT.Copy).then_inc(S["B_whc"], 1)

            def slope(chain, dst, src, alpha):
                def step(g):
                    done(act, chain + "_s", g)
                    act.activation(dst, src, ACT.Copy, scale=alpha).then_inc(S[chain + "_slope"], 1)
                return step

            def exp_and_sum(chain, t, minus_max, total):
                def step(g):
                    done(act, chain + "_max", g)
                    act.activation(t[:, :], t[:, :], ACT.Exp, bias=minus_max[:, :], accum_out=total[:, :])\
                       .then_inc(S[chain + "_exp"], 1)
                return step

            def C_oexp(g):
                done(act, "C_o", g)
                done(act, "C_recip", g)
                act.activation(C_e[:, :], pC[:, 0:D], ACT.Exp, scale=C_rec[:, :]).then_inc(S["C_oexp"], 1)

            def C_hidc(g):
                done(act, "C_hid", g)
                act.activation(C_hid[:, 0:P], pC[:, 0:P], ACT.Relu, bias=b1_c[:, 0:1])
                act.activation(C_hid[:, P:D], pC[:, P:D], ACT.Relu, bias=b1_c[:, 1:2]).then_inc(S["C_hidc"], 1)

            def D_kc(g):
                done(act, "D_kv", g)
                done_before(act, "D_klow", g)
                for c in range(K):
                    last = act.activation(D_k[:, c, :], pB[:, 1, c * P:(c + 1) * P], ACT.Identity, bias=bk_c[:, c:c + 1])
                last.then_inc(S["D_kc"], 1)

            def D_qc(g):
                done(act, "D_q", g)
                done_before(act, "D_qlow", g)
                for c in range(K):
                    last = act.activation(D_q[:, c * P:(c + 1) * P], pB[:, 1, c * P:(c + 1) * P], ACT.Identity,
                                          bias=bq_c[:, c:c + 1], scale=SCALE)
                last.then_inc(S["D_qc"], 1)

            def D_qhigh(g):
                done(act, "D_qc", g)
                done_before(act, "F_s", g)
                act.activation(D_qhl[0][:, :], D_q[:, :], ACT.Copy).then_inc(S["D_qhigh"], 1)

            def F_exp(g):
                done(act, "F_max", g)
                for h in range(HEADS_L1):
                    last = act.activation(F_s[:, h, :], pF[:, h // HPC, (h % HPC) * P:(h % HPC + 1) * P], ACT.Exp,
                                          bias=F_m[:, h:h + 1])
                last.then_inc(S["F_exp"], 1)

            def E_hc(g):
                done(act, "E_h", g)
                done_before(act, "E_right", g)
                act.activation(E_h[:, :], pE[:, 0:F3 + 2], ACT.Copy).then_inc(S["E_hc"], 1)

            rounds(act, ACT_ORDER, {
                "A_hT": relu_copy("A_zT", "A_hT", A_hT[:, :], pA[:, 0, 0:D]),
                "A_whc_hi": A_whc_hi, "A_whc_lo": A_whc_lo, "A_slope": A_slope, "A_exp": A_exp, "A_attn": A_attn,
                "A_fc": copy("A_f", "A_fc", A_f[:, :], pA[:, 0, 0:2 * H0]),
                "A_high": copy("A_hT", "A_high", A_hl[0][:, :], A_hT[:, :]),
                "B_exp": B_exp, "B_high": copy("B_h", "B_high", B_hl[0][:, :], B_e[:, :]), "B_whc": B_whc,
                "C_slope": slope("C", C_l[:, :], pC[:, 0:P], SLOPE_L0),
                "C_exp": exp_and_sum("C", C_l, C_m, C_sum),
                "C_attn": copy("C_pT", "C_attn", C_aT[:, :], pC[:, P:2 * P]),
                "C_oexp": C_oexp,
                "C_hTc": copy("C_hT", "C_hTc", C_hT[:, :], pC[:, D:2 * D]),
                "C_hidc": C_hidc, "C_high": copy("C_hidc", "C_high", C_hl[0][:, :], C_hid[:, :]),
                "D_hT": relu_copy("D_zT", "D_hT", D_hT[:, :], pB[:, 1, 0:D]),
                "D_high": copy("D_hT", "D_high", D_hl[0][:, :], D_hT[:, :]),
                "D_kc": D_kc, "D_qc": D_qc, "D_qhigh": D_qhigh, "F_exp": F_exp,
                "F_pTc": copy("F_pT", "F_pTc", F_pT[:, :, :].rearrange("p h n -> p (h n)"),
                              pF[:, :, :].rearrange("p b n -> p (b n)")),
                "F_high": copy("F_oT", "F_high", F_hl[0][:, :], pF[:, 1, 0:D]),
                "E_high": relu_copy("E_z", "E_high", E_hl[0][:, :], E_z[:, :]),
                "E_ahhigh": copy("E_ah", "E_ahhigh", E_ahl[0][:, :], pE[:, :]),
                "E_hT3": relu_copy("E_zT3", "E_hT3", E_hT[:, :], pE[:, D:2 * D]),
                "E_hc": E_hc,
                "E_slope": slope("E", E_l[:, :], pE[:, 384:512], SLOPE_L3),
                "E_exp": exp_and_sum("E", E_l, E_m, E_sum),
                "E_attn": copy("E_pT", "E_attn", E_aT[:, :], pE[:, 256:384]),
            })

        @block.vector
        def _(dve):
            dve.wait_ge(weights_loaded, LOADED)
            dve.wait_ge(consts_built, BUILT)
            dve.tensor_copy(adj_f[:, :], adj_i[:, :]).then_inc(adj_ready, 1)
            dve.wait_ge(adj_ready, 1)
            dve.tensor_reduce(deg[:, :], adj_f[:, :], AX.X, ALU.add).then_inc(dve_setup, 1)
            dve.tensor_scalar(products[:, 0:P], adj_f[:, :], 0.0, -1.0, ALU.is_gt, ALU.add).then_inc(deg_ready, 1)
            dve.wait_ge(deg_ready, 1)
            dve.tensor_scalar(mask[:, :], products[:, 0:P], -MASKED, None, ALU.mult).then_inc(dve_setup, 1)
            dve.tensor_copy(ident_bf[:, :], ident[:, :]).then_inc(dve_setup, 1)
            dve.tensor_scalar(bq_c[:, :], bq_c[:, :], SCALE, None, ALU.mult).then_inc(bq_scaled, 1)
            dve.wait_ge(dve_setup, 3)
            dve.tensor_scalar(deg_bl2[:, :], bl2_b[:, :], deg[:, 0:1], None, ALU.mult).then_inc(dve_setup, 1)
            dve.tensor_scalar(adj_deg[:, P:2 * P], ident[:, :], deg[:, 0:1], None, ALU.mult).then_inc(dve_setup, 1)
            count = 5
            dots = [(wh_w[:, c, h, :], a0_b[:, h, t * D:(t + 1) * D], wa_w[:, c, t * H0 + h:t * H0 + h + 1])
                    for c in range(K) for h in range(H0) for t in range(2)]
            dots += [(wout_w[:, c, 0:D], aout_b[:, t * D:(t + 1) * D], wout_w[:, c, D + t:D + t + 1])
                     for c in range(KH) for t in range(2)]
            dots += [(w3_w[:, c, 0:F3], a3_b[:, t * F3:(t + 1) * F3], w3_w[:, c, F3 + t:F3 + t + 1])
                     for c in range(K) for t in range(2)]
            for w, a, dot in dots:
                dve.tensor_tensor_reduce(products[:, 0:a.shape[1]], w, a, 1.0, 0.0, ALU.mult, ALU.add, dot)\
                   .then_inc(dve_setup, 1)
                count += 1
                dve.wait_ge(dve_setup, count)
            dve.wait_ge(adjT_done, 1)
            dve.tensor_copy(adj_deg[:, 0:P], pA[:, 0, 0:P]).then_inc(dve_setup, 1)
            count += 1
            splits = [(wh_w, wh_hl), (wout_w, wout_hl), (w2_w, w2_hl), (wv_w, wv_hl), (wo_w, wo_hl), (wij_w, wij_hl)]
            flat = lambda t: t[:, :, :, :].rearrange("p k h d -> p (k h d)") if len(t.shape) == 4 \
                else t[:, :, :].rearrange("p k d -> p (k d)")
            for w, (high, low) in splits:
                dve.tensor_copy(flat(high), flat(w)).then_inc(dve_setup, 1)
                count += 1
            dve.wait_ge(dve_setup, count)
            for w, (high, low) in splits:
                dve.tensor_tensor(flat(low), flat(w), flat(high).bitcast(F32), ALU.subtract).then_inc(dve_setup, 1)
                count += 1
            assert count == DVE_SETUP

            def stats(chain, suffix, x, st, after):
                def step(g):
                    dve.wait_ge(consts_built, BUILT)
                    after(g)
                    dve.bn_stats(st[:, :], x(g)).then_inc(S[chain + "_stats" + suffix], 1)
                return step

            def moments(chain, suffix, st, mv):
                def step(g):
                    done_apart(dve, chain + "_stats" + suffix, g)
                    dve.bn_aggr(mv[:, :], st[:, :]).then_inc(S[chain + "_moments" + suffix], 1)
                return step

            def normalise(chain, suffix, z, mv, rs):
                def step(g):
                    done(dve, chain + "_rstd" + suffix, g)
                    dve.tensor_scalar(z[:, :], slot(g), mv[:, 0:1], rs[:, 0:1], ALU.subtract, ALU.mult)\
                       .then_inc(S[chain + "_z" + suffix], 1)
                return step

            def copy(after, signal, dst, src):
                def step(g):
                    done(dve, after, g)
                    dve.tensor_copy(dst, src).then_inc(S[signal], 1)
                return step

            def low_part(after, signal, hl, x, cols):
                def step(g):
                    done(dve, after, g)
                    dve.tensor_tensor(hl[1][:, cols], x[:, cols], hl[0][:, cols].bitcast(F32), ALU.subtract)\
                       .then_inc(S[signal], 1)
                return step

            def A_leaky(g):
                done(dve, "A_slope", g)
                flat = A_l[:, :, :].rearrange("p h m -> p (h m)")
                dve.tensor_tensor(flat, pA[:, 0, :], flat, ALU.max).then_inc(S["A_leaky"], 1)

            def A_max(g):
                done(dve, "A_leaky", g)
                dve.tensor_reduce(A_m[:, :], A_l[:, :, :], AX.X, ALU.max, negate=True).then_inc(S["A_max"], 1)

            def A_norm(g):
                done(dve, "A_recip", g)
                dve.tensor_tensor(A_l[:, :, :], A_l[:, :, :], A_rec[:, :].unsqueeze(2).to_broadcast([P, H0, P]), ALU.mult)\
                   .then_inc(S["A_norm"], 1)

            def B_h(g):
                done(dve, "B_exp", g)
                dve.scalar_tensor_tensor(out=B_e[:, :], in0=B_e[:, :], scalar=-1.0,
                                         in1=pB[:, :, :].rearrange("p b n -> p (b n)"),
                                         op0=ALU.add, op1=ALU.max).then_inc(S["B_h"], 1)

            def leaky(chain, t, scores):
                def step(g):
                    done(dve, chain + "_slope", g)
                    dve.tensor_tensor(t[:, :], scores, t[:, :], ALU.max).then_inc(S[chain + "_leaky"], 1)
                return step

            def minus_max(chain, m, t):
                def step(g):
                    done(dve, chain + "_leaky", g)
                    dve.tensor_reduce(m[:, :], t[:, :], AX.X, ALU.max, negate=True).then_inc(S[chain + "_max"], 1)
                return step

            def recip(chain, r, total):
                def step(g):
                    done(dve, chain + "_exp", g)
                    dve.reciprocal(r[:, :], total[:, :]).then_inc(S[chain + "_recip"], 1)
                return step

            def C_min(g):
                done(dve, "C_oexp", g)
                dve.tensor_scalar(C_e[:, :], C_e[:, :], 1.0, -1.0, ALU.min, ALU.add).then_inc(S["C_min"], 1)

            def C_h_step(g):
                done(dve, "C_min", g)
                done_before(dve, "C_hb", g)
                dve.scalar_tensor_tensor(out=C_h[:, :], in0=pC[:, 0:D], scalar=C_rec[:, :], in1=C_e[:, :],
                                         op0=ALU.mult, op1=ALU.max).then_inc(S["C_h"], 1)

            def C_y_step(g):
                done(dve, "C_ffn", g)
                done(dve, "C_hb", g)
                dve.tensor_tensor(C_y[:, :], pC[:, D:2 * D], C_hb[:, :], ALU.add).then_inc(S["C_y"], 1)

            def C_g_step(g):
                done(dve, "C_moments", g)
                dve.scalar_tensor_tensor(out=C_g[:, :], in0=C_y[:, :], scalar=C_mv[:, 0:1], in1=gamma_b[:, :],
                                         op0=ALU.subtract, op1=ALU.mult).then_inc(S["C_g"], 1)

            def C_x1(g):
                done(dve, "C_g", g)
                done(dve, "C_rstd", g)
                done(dve, "C_xb", g)
                dve.scalar_tensor_tensor(out=slot(g), in0=C_g[:, :], scalar=C_rs[:, 0:1], in1=slot(g),
                                         op0=ALU.mult, op1=ALU.add).then_inc(S["C_x1"], 1)

            def own_block(t, h):
                return t[h * DH:(h + 1) * DH, :, h, :]

            def D_khigh(g):
                done(dve, "D_kc", g)
                done_before(dve, "F_s", g)
                for h in range(HPC):
                    last = dve.tensor_copy(own_block(D_khl[0], h), D_k[h * DH:(h + 1) * DH, :, :])
                last.then_inc(S["D_khigh"], 1)

            def D_klow(g):
                done(dve, "D_khigh", g)
                for h in range(HPC):
                    last = dve.tensor_tensor(own_block(D_khl[1], h), D_k[h * DH:(h + 1) * DH, :, :],
                                             own_block(D_khl[0], h).bitcast(F32), ALU.subtract)
                last.then_inc(S["D_klow"], 1)

            def D_vc(g):
                done(dve, "D_kc", g)
                done_before(dve, "F_o", g)
                heads = lambda t: t.rearrange("p (h d) -> p h d", h=HEADS_L1)
                dve.tensor_tensor(D_v[:, 0:HEADS_L1, 0:DH], heads(pB[:, 1, D:2 * D]), heads(bv_b[:, :]), ALU.add)\
                   .then_inc(S["D_vc"], 1)

            def F_max(g):
                done(dve, "F_s", g)
                s = pF[:, :, :].rearrange("p b (h n) -> p (b h) n", n=P)
                dve.tensor_reduce(F_m[:, :], s, AX.X, ALU.max, negate=True).then_inc(S["F_max"], 1)

            def F_recip(g):
                done(dve, "F_o", g)
                o = pF[:, :, :].rearrange("p b (h d) -> p (b h) d", d=P)
                dve.reciprocal(F_rec[:, :].unsqueeze(2), o[:, :, DH:DH + 1]).then_inc(S["F_recip"], 1)

            def F_on(g):
                done(dve, "F_recip", g)
                o = pF[:, :, :].rearrange("p b (h d) -> p (b h) d", d=P)
                dve.tensor_tensor(F_o[:, :].rearrange("p (h d) -> p h d", h=HEADS_L1), o[:, :, 0:DH],
                                  F_rec[:, :].unsqueeze(2).to_broadcast([P, HEADS_L1, DH]), ALU.mult)\
                   .then_inc(S["F_on"], 1)

            def F_x2(g):
                done(dve, "F_out", g)
                done(dve, "D_xb", g)
                dve.tensor_tensor(slot(g), pF[:, 1, D:2 * D], slot(g), ALU.add).then_inc(S["F_x2"], 1)

            def E_low_step(g):
                done(dve, "E_high", g)
                dve.scalar_tensor_tensor(out=E_hl[1][:, :], in0=E_z[:, :], scalar=0.0, in1=E_hl[0][:, :].bitcast(F32),
                                         op0=ALU.max, op1=ALU.subtract).then_inc(S["E_low"], 1)

            def E_x3(g):
                done(dve, "E_m", g)
                done(dve, "E_xb", g)
                dve.tensor_tensor(slot(g), pE[:, 0:D], slot(g), ALU.add).then_inc(S["E_x3"], 1)

            def E_left(g):
                done(dve, "E_o", g)
                done(dve, "E_recip", g)
                left = xs[:, g % SLOTS, 0:F3]
                dve.scalar_tensor_tensor(out=left, in0=pE[:, 384:512], scalar=E_rec[:, :], in1=left,
                                         op0=ALU.mult, op1=ALU.add).then_inc(S["E_left"], 1)

            rounds(dve, DVE_ORDER, {
                "A_stats": stats("A", "", slot, A_st, lambda g: dve.wait_ge(x_loaded, 16 * (g + 1))),
                "A_moments": moments("A", "", A_st, A_mv), "A_z": normalise("A", "", A_z, A_mv, A_rs),
                "A_fTc": copy("A_fT", "A_fTc", A_fT[0:3 * 2 * H0, :], pA[0:3 * 2 * H0, 1, 0:P // 2].bitcast(BF16)),
                "A_leaky": A_leaky, "A_max": A_max, "A_recip": recip("A", A_rec, A_sum), "A_norm": A_norm,
                "B_h": B_h, "B_low": low_part("B_high", "B_low", B_hl, B_e, slice(0, HD // 2)),
                "C_fTc": copy("C_fT", "C_fTc", C_fT[0:6, :], pC[0:6, D:D + P // 2].bitcast(BF16)),
                "C_leaky": leaky("C", C_l, pC[:, 0:P]), "C_max": minus_max("C", C_m, C_l),
                "C_recip": recip("C", C_rec, C_sum), "C_min": C_min, "C_h": C_h_step, "C_y": C_y_step,
                "C_stats": stats("C", "", lambda g: C_y[:, :], C_st, lambda g: done(dve, "C_y", g)),
                "C_moments": moments("C", "", C_st, C_mv), "C_g": C_g_step, "C_x1": C_x1,
                "D_stats": stats("D", "", slot, D_st, lambda g: done(dve, "C_x1", g)),
                "D_moments": moments("D", "", D_st, D_mv), "D_z": normalise("D", "", D_z, D_mv, D_rs),
                "D_khigh": D_khigh, "D_klow": D_klow, "D_vc": D_vc, "F_max": F_max, "F_recip": F_recip, "F_on": F_on,
                "F_low": low_part("F_high", "F_low", F_hl, pF[:, 1, :], slice(0, D)), "F_x2": F_x2,
                "E_stats": stats("E", "", slot, E_st, lambda g: done(dve, "F_x2", g)),
                "E_moments": moments("E", "", E_st, E_mv), "E_z": normalise("E", "", E_z, E_mv, E_rs),
                "E_low": E_low_step, "E_ahlow": low_part("E_ahhigh", "E_ahlow", E_ahl, pE, slice(0, 2 * D)),
                "E_x3": E_x3,
                "E_stats3": stats("E", "3", slot, E_st, lambda g: done(dve, "E_x3", g)),
                "E_moments3": moments("E", "3", E_st, E_mv), "E_z3": normalise("E", "3", E_z, E_mv, E_rs),
                "E_fTc": copy("E_fT", "E_fTc", E_fT[0:6, :], pE[0:6, 256:256 + P // 2].bitcast(BF16)),
                "E_leaky": leaky("E", E_l, pE[:, 384:512]), "E_max": minus_max("E", E_m, E_l),
                "E_recip": recip("E", E_rec, E_sum), "E_left": E_left,
            })

        @block.tensor
        def _(pe):
            pe.wait_ge(consts_built, BUILT)
            pe.wait_ge(adj_ready, 1)
            pe.transpose(pA[:, 0, 0:P], adj_f[:, :], ident[:, :]).then_inc(adjT_done, 1)
            pe.wait_ge(weights_loaded, LOADED)
            pe.wait_ge(dve_setup, DVE_SETUP)

            def transposes(dst, src, n):
                for j in range(n):
                    last = pe.transpose(dst[:, j * P:(j + 1) * P], src[:, j * P:(j + 1) * P], ident[:, :])
                return last

            def add_mask(dst, heads):
                m = mask[:, :] if heads == 1 else mask[:, :].unsqueeze(1).to_broadcast([P, heads, P])
                pe.matmul(dst, ident_bf[:, :], m, start=True, stop=False)

            def project(dst, hT, w):
                for k in range(K):
                    last = pe.matmul(dst, hT[:, k * P:(k + 1) * P], w[:, k, :], start=(k == 0), stop=(k == K - 1))
                return last

            def split_product(dst, parts, opens=True):
                terms = []
                for a_high, a_low, b_high, b_low in parts:
                    terms += [(a_high, b_high), (a_high, b_low), (a_low, b_high)]
                for i, (a, b) in enumerate(terms):
                    last = pe.matmul(dst, a, b, start=(opens and i == 0), stop=(i == len(terms) - 1))
                return last

            def split_project(dst, hl, w_hl):
                return split_product(dst, [(hl[0][:, k * P:(k + 1) * P], hl[1][:, k * P:(k + 1) * P],
                                            w_hl[0][:, k, :], w_hl[1][:, k, :]) for k in range(K)])

            def A_zT(g):
                done(pe, "A_z", g)
                done_before(pe, "A_attn", g)
                transposes(pA[:, 0, :], A_z, K).then_inc(S["A_zT"], 1)

            def A_f(g):
                done(pe, "A_hT", g)
                project(pA[:, 0, 0:P], A_hT, wa_w).then_inc(S["A_f"], 1)

            def A_wh_hi(g):
                done(pe, "A_low", g)
                wh = [w[:, :, 2:4, :].rearrange("p k h d -> p k (h d)") for w in wh_hl]
                split_project(pA[:, 1, :], A_hl, wh).then_inc(S["A_wh_hi"], 1)

            def A_wh_lo(g):
                done(pe, "A_fc", g)
                wh = [w[:, :, 0:2, :].rearrange("p k h d -> p k (h d)") for w in wh_hl]
                split_project(pA[:, 0, :], A_hl, wh).then_inc(S["A_wh_lo"], 1)

            def logits_transposed(dst, f3):
                n = f3.shape[1]
                return pe.transpose(dst[0:n, 0:P // 2].bitcast(BF16), f3[:, :], ident_bf[:, :])

            def A_fT_step(g):
                done(pe, "A_fcopy", g)
                done(pe, "A_whc_hi", g)
                logits_transposed(pA[:, 1, :], A_f3).then_inc(S["A_fT"], 1)

            def A_s(g):
                done(pe, "A_fTc", g)
                done(pe, "A_whc_lo", g)
                add_mask(pA[:, 0, :].rearrange("p (h m) -> p h m", h=H0), H0)
                pe.matmul(pA[:, 0, :], A_fT[:, :], pick0[:, 0:H0, :].rearrange("r h m -> r (h m)"), start=False, stop=False)
                for h in range(H0):
                    last = pe.matmul(pA[:, 0, h * P:(h + 1) * P], pick0[:, H0 + h, :], A_fT[:, :],
                                     start=False, stop=(h == H0 - 1))
                last.then_inc(S["A_s"], 1)

            def A_pT(g):
                done(pe, "A_norm", g)
                transposes(pA[:, 1, :], A_l[:, :, :].rearrange("p h m -> p (h m)"), H0).then_inc(S["A_pT"], 1)

            def B_o(g):
                done(pe, "A_attn", g)
                done_before(pe, "B_whc", g)
                done_in_round(pe, "D_qc", "B", g, 1)
                for k in range(KH):
                    h, c = k // K, k % K
                    last = pe.matmul(pB[:, k // 4, (k % 4) * P:(k % 4 + 1) * P], whs[:, h, c * P:(c + 1) * P],
                                     attnT[:, h, :], start=True, stop=True)
                last.then_inc(S["B_o"], 1)

            def B_wh(part):
                def step(g):
                    if part == 0:
                        done(pe, "B_low", g)
                    if part == 2:
                        done(pe, "B_low2", g)
                    for k in range(part * KH // 4, (part + 1) * KH // 4):
                        high, low = (t[:, k * P:(k + 1) * P] for t in B_hl)
                        for i, (a, w) in enumerate(((high, wout_hl[0]), (high, wout_hl[1]), (low, wout_hl[0]))):
                            last = pe.matmul(pB[:, 0, 0:D + 2], a, w[:, k, :],
                                             start=(k == 0 and i == 0), stop=(k == KH - 1 and i == 2))
                    if part == 3:
                        last.then_inc(S["B_wh"], 1)
                return step

            def C_fT_step(g):
                done(pe, "C_fcopy", g)
                done_before(pe, "C_y", g)
                logits_transposed(pC[:, D:2 * D], C_f3).then_inc(S["C_fT"], 1)

            def one_head(dst, fT, signal):
                add_mask(dst, 1)
                pe.matmul(dst, fT[:, :], pick[:, 0, :], start=False, stop=False)
                pe.matmul(dst, pick[:, 1, :], fT[:, :], start=False, stop=True).then_inc(S[signal], 1)

            def C_s(g):
                done(pe, "C_fTc", g)
                one_head(pC[:, 0:P], C_fT, "C_s")

            def C_pT(g):
                done(pe, "C_exp", g)
                pe.transpose(pC[:, P:2 * P], C_l[:, :], ident[:, :]).then_inc(S["C_pT"], 1)

            def C_o(g):
                done(pe, "C_attn", g)
                pe.matmul(pC[:, 0:D], C_aT[:, :], wh2[:, 0:D], start=True, stop=True).then_inc(S["C_o"], 1)

            def C_hT_step(g):
                done(pe, "C_h", g)
                transposes(pC[:, D:2 * D], C_h, K).then_inc(S["C_hT"], 1)

            def transposed_product(dst, w, hT):
                for c in range(K):
                    for k in range(K):
                        last = pe.matmul(dst[:, c * P:(c + 1) * P], w[:, k, c * P:(c + 1) * P], hT[:, k * P:(k + 1) * P],
                                         start=(k == 0), stop=(k == K - 1))
                return last

            def C_hid_step(g):
                done(pe, "C_hTc", g)
                transposed_product(pC[:, 0:D], w1_w, C_hT).then_inc(S["C_hid"], 1)

            def C_ffn(g):
                done(pe, "C_low", g)
                split_project(pC[:, D:2 * D], C_hl, w2_hl).then_inc(S["C_ffn"], 1)

            def D_zT(g):
                done(pe, "D_z", g)
                done_in_round(pe, "B_h", "D", g)
                transposes(pB[:, 1, :], D_z, K).then_inc(S["D_zT"], 1)

            def D_q_step(g):
                done(pe, "D_vc", g)
                transposed_product(pB[:, 1, 0:D], wq_w, D_hT).then_inc(S["D_q"], 1)

            def D_k_step(g):
                done(pe, "D_hT", g)
                transposed_product(pB[:, 1, 0:D], wk_w, D_hT)

            def D_v_step(g):
                done(pe, "D_low", g)
                split_project(pB[:, 1, D:2 * D], D_hl, wv_hl).then_inc(S["D_kv"], 1)

            def F_s_step(c):
                def step(g):
                    if c == 0:
                        done(pe, "D_klow", g)
                        done(pe, "D_qlow", g)
                        done_before(pe, "F_x2", g)
                    add_mask(pF[:, c, :].rearrange("p (h m) -> p h m", h=HPC), HPC)
                    q_high, q_low = (t[:, c * P:(c + 1) * P] for t in D_qhl)
                    k_high, k_low = (t[:, c, :, :].rearrange("p h m -> p (h m)") for t in D_khl)
                    last = split_product(pF[:, c, :], [(q_high, q_low, k_high, k_low)], opens=False)
                    if c == K - 1:
                        last.then_inc(S["F_s"], 1)
                return step

            def F_pT_step(g):
                done(pe, "F_exp", g)
                transposes(pF[:, :, :].rearrange("p b n -> p (b n)"), F_s[:, :, :].rearrange("p h m -> p (h m)"), HEADS_L1)\
                    .then_inc(S["F_pT"], 1)

            def F_o_step(c):
                def step(g):
                    if c == 0:
                        done(pe, "D_vc", g)
                        done(pe, "F_pTc", g)
                    v = D_v[:, :, :].rearrange("p h d -> p (h d)")
                    for h in range(c * HPC, (c + 1) * HPC):
                        last = pe.matmul(pF[:, c, (h % HPC) * P:(h % HPC + 1) * P], F_pT[:, h, :],
                                         v[:, h * (DH + 1):h * (DH + 1) + P], start=True, stop=True)
                    if c == K - 1:
                        last.then_inc(S["F_o"], 1)
                return step

            def F_oT_step(g):
                done(pe, "F_on", g)
                transposes(pF[:, 1, :], F_o, K).then_inc(S["F_oT"], 1)

            def F_out(g):
                done(pe, "F_low", g)
                split_project(pF[:, 1, D:2 * D], F_hl, wo_hl).then_inc(S["F_out"], 1)

            def E_ah(g):
                done(pe, "E_low", g)
                done_before(pe, "E_left", g)
                for c in range(K):
                    for i, h in enumerate(E_hl):
                        last = pe.matmul(pE[:, c * D:(c + 1) * D], h[:, c * P:(c + 1) * P], adj_deg[:, :],
                                         start=(i == 0), stop=(i == 1))
                last.then_inc(S["E_ah"], 1)

            def E_m(g):
                done(pe, "E_ahlow", g)
                split_product(pE[:, 0:D], [(*(t[:, c * D + side * P:c * D + (side + 1) * P] for t in E_ahl),
                                            *(w[:, c, (1 - side) * D:(2 - side) * D] for w in wij_hl))
                                           for c in range(K) for side in range(2)]).then_inc(S["E_m"], 1)

            def E_zT3(g):
                done(pe, "E_z3", g)
                transposes(pE[:, D:2 * D], E_z, K).then_inc(S["E_zT3"], 1)

            def E_h_step(g):
                done(pe, "E_hT3", g)
                project(pE[:, 0:F3 + 2], E_hT, w3_w).then_inc(S["E_h"], 1)

            def E_fT_step(g):
                done(pe, "E_fcopy", g)
                logits_transposed(pE[:, 256:384], E_f3).then_inc(S["E_fT"], 1)

            def E_s(g):
                done(pe, "E_fTc", g)
                one_head(pE[:, 384:512], E_fT, "E_s")

            def E_pT(g):
                done(pe, "E_exp", g)
                pe.transpose(pE[:, 256:384], E_l[:, :], ident[:, :]).then_inc(S["E_pT"], 1)

            def E_o(g):
                done(pe, "E_attn", g)
                pe.matmul(pE[:, 384:512], E_aT[:, :], E_h[:, 0:F3], start=True, stop=True).then_inc(S["E_o"], 1)

            rounds(pe, PE_ORDER, {
                "A_zT": A_zT, "A_f": A_f, "A_wh_hi": A_wh_hi, "A_wh_lo": A_wh_lo, "A_fT": A_fT_step, "A_s": A_s, "A_pT": A_pT,
                "B_o": B_o, "B_wh.0": B_wh(0), "B_wh.1": B_wh(1), "B_wh.2": B_wh(2),
                "B_wh": B_wh(3),
                "C_fT": C_fT_step, "C_s": C_s, "C_pT": C_pT, "C_o": C_o, "C_hT": C_hT_step, "C_hid": C_hid_step,
                "C_ffn": C_ffn,
                "D_zT": D_zT, "D_q": D_q_step, "D_k.0": D_k_step, "D_kv": D_v_step, "F_s.0": F_s_step(0), "F_s": F_s_step(1),
                "F_pT": F_pT_step, "F_o.0": F_o_step(0), "F_o": F_o_step(1), "F_oT": F_oT_step, "F_out": F_out,
                "E_ah": E_ah, "E_m": E_m, "E_zT3": E_zT3, "E_h": E_h_step, "E_fT": E_fT_step, "E_s": E_s,
                "E_pT": E_pT, "E_o": E_o,
            })


def kernel(**inputs):
    import numpy as np
    import concourse.bacc as bacc
    from concourse import mybir as mb
    from concourse.bass_utils import run_bass_kernel_spmd as run

    def transposed(a):
        return np.ascontiguousarray(np.asarray(a).T)

    def columns(a):
        return transposed(np.asarray(a).reshape(-1, 128))

    plain = lambda name: np.ascontiguousarray(np.asarray(inputs[name]))
    w_l2 = plain("L2_gnn_W")
    d = w_l2.shape[0]
    arrays = {
        "x": plain("x"), "adj": plain("adj"),
        "w_heads": plain("L0_gnn_W_heads"), "a_heads": plain("L0_gnn_a_heads"),
        "w_out": plain("L0_gnn_W_out"), "a_out": plain("L0_gnn_a_out"),
        "w1": plain("L0_gnn_w1"), "b1": columns(inputs["L0_gnn_b1"]), "w2": plain("L0_gnn_w2"), "b2": plain("L0_gnn_b2"),
        "gamma": plain("L0_gnn_ln_gamma"), "beta": plain("L0_gnn_ln_beta"),
        "wqT": transposed(inputs["L1_gnn_Wq"]), "bq": columns(inputs["L1_gnn_bq"]),
        "wkT": transposed(inputs["L1_gnn_Wk"]), "bk": columns(inputs["L1_gnn_bk"]),
        "wvT": transposed(inputs["L1_gnn_Wv"]), "bv": plain("L1_gnn_bv"),
        "woT": transposed(inputs["L1_gnn_Wo"]), "bo": plain("L1_gnn_bo"),
        "wijT": np.ascontiguousarray(np.concatenate([w_l2[:, :d].T, w_l2[:, d:].T], axis=1)),
        "b_l2": plain("L2_gnn_b"),
        "w_l3": plain("L3_gnn_W"), "a_l3": plain("L3_gnn_a"),
    }
    nc = bacc.Bacc("TRN2", target_bir_lowering=False, num_devices=1)
    args = [nc.dram_tensor(f"in_{n}", a.shape, mb.dt.from_np(a.dtype), kind="ExternalInput").ap()
            for n, a in arrays.items()]
    out = nc.dram_tensor("out_x", arrays["x"].shape, mb.dt.float32, kind="ExternalOutput").ap()
    gnn_stack(nc, *args, out)
    r = run(nc, [{f"in_{n}": a for n, a in arrays.items()}], core_ids=[0])
    return r.results[0]["out_x"]
```

```python
import concourse.bass as bass
from concourse import mybir
from contextlib import ExitStack

ALU = mybir.AluOpType
ACT = mybir.ActivationFunctionType
AX = mybir.AxisListType
F32 = mybir.dt.float32
BF16 = mybir.dt.bfloat16
F32R = mybir.dt.float32r
I32 = mybir.dt.int32

EPS = 1e-5
MASKED = -1e11
HUGE = 3e38
SLOPE_L0 = 0.01
SLOPE_L3 = 0.2
HEADS_L1 = 8
UNROLLED = 4
SLOTS = 8

CHAINS = "ABCDFE"

PE_ORDER = """
F_s.0 B_o.0 C_fT B_o C_s A_zT F_s F_pT.0 A_f E_ah C_pT A_wh_hi C_o E_m D_zT A_wh_lo A_fT F_o.0 D_k.0 A_s C_hT
E_zT3 F_pT D_kv E_h C_hid B_wh.0 F_o E_fT B_wh.1 E_s C_ffn F_oT D_q B_wh.2 E_pT F_out A_pT E_o B_wh
""".split()
ACT_ORDER = """
F_exp.0 C_slope A_hT E_high A_high C_exp B_neg A_fc E_ahhigh C_attn B_exp B_neg.0 B_exp.0 A_whc_hi C_oexp
F_pTc.0 B_high.0 D_hT D_high A_whc_lo F_exp A_slope C_hTc E_hT3 F_pTc D_kc E_hc B_high C_hidc C_high A_exp
E_slope F_high E_exp D_qc D_qhigh E_attn A_attn B_whc
""".split()
DVE_ORDER = """
E_stats A_stats E_moments A_moments F_max.0 C_fTc A_z E_z C_leaky C_max E_low D_stats C_recip F_max E_ahlow
D_moments B_h D_z B_h.0 E_x3 C_min E_stats3 E_moments3 A_fTc C_h B_low.0 E_z3 A_leaky A_max D_khigh D_klow
F_recip E_fTc F_on D_vc E_leaky A_recip C_y E_max C_stats F_low C_moments A_norm E_recip C_g C_x1 F_x2 E_left
""".split()
POOL_ORDER = """
C_fcopy A_rstd E_rstd A_low D_rstd E_xb A_fcopy E_rstd3 D_low C_hb D_xb C_xb E_fcopy C_low B_low C_rstd D_qlow
E_right
""".split()

STEP_SEMAPHORES = """
A_stats A_moments A_var A_rstd A_z A_zT A_hT A_high A_low A_f A_fc A_fparts A_fcopy A_wh_hi A_wh_lo A_whc_hi
A_whc_lo A_fT A_fTc A_s A_slope A_leaky A_max A_exp A_recip A_norm A_pT A_attn
B_o0 B_o B_neg0 B_neg B_exp0 B_exp B_h0 B_h B_high0 B_high B_low0 B_low B_wh B_whc
C_fparts C_fcopy C_fT C_fTc C_s C_slope C_leaky C_max C_exp C_recip C_pT C_attn C_o C_oexp C_min C_h C_hb C_hT
C_hTc C_hid C_hidc C_high C_low C_ffn C_y C_stats C_moments C_var C_rstd C_xb C_g C_x1
D_stats D_moments D_var D_rstd D_z D_xb D_zT D_hT D_high D_low D_kv D_kc D_khigh D_klow D_vc D_q D_qc D_qhigh
D_qlow
F_s0 F_s F_max0 F_max F_exp0 F_exp F_pT0 F_pT F_pTc0 F_pTc F_o F_recip F_on F_oT F_high F_low F_out F_x2
E_stats E_moments E_var E_rstd E_z E_high E_low E_xb E_ah E_ahhigh E_ahlow E_m E_x3 E_stats3 E_moments3
E_rstd3 E_z3 E_zT3 E_hT3 E_h E_hc E_fparts E_fcopy E_fT E_fTc E_s E_slope E_leaky E_max E_exp E_recip E_pT
E_attn E_o E_left E_right
""".split()


def gnn_stack(nc, x, adj, w_heads, a_heads, w_out, a_out, w1, b1, w2, b2, gamma, beta,
              wqT, bq, wkT, bk, wvT, bv, woT, bo, wijT, b_l2, w_l3, a_l3, out):
    GRAPHS, N, D = x.shape
    P = 128
    assert N == P and D == 2 * P
    K = D // P
    H0 = w_heads.shape[0]
    HD = H0 * D
    KH = HD // P
    DH = D // HEADS_L1
    HPC = P // DH
    F3 = w_l3.shape[1]
    SCALE = float(DH) ** -0.5

    with ExitStack() as ctx:
        def sb(name, shape, dt=F32):
            return ctx.enter_context(nc.sbuf_tensor(name, shape, dt))

        def ps(name, shape):
            return ctx.enter_context(nc.psum_tensor(name, shape, F32))

        def sem(name):
            return ctx.enter_context(nc.semaphore(name))

        ident = sb("ident", [P, P])
        ident_bf = sb("ident_bf", [P, P], BF16)
        HALF = 32
        pick0 = sb("pick0", [P, H0, P], BF16)
        pick = sb("pick", [P, 2, P], BF16)
        adj_i = sb("adj_i", [P, P], I32)
        adj_f = sb("adj_f", [P, P])
        adj_deg = sb("adj_deg", [P, 2 * P], F32R)
        mask = sb("mask", [P, P])
        deg = sb("deg", [P, 1])
        minus_half = sb("minus_half", [P, 1])
        eps = sb("eps", [P, 1])
        zeros = sb("zeros", [P, 2 * H0])
        PRODUCTS = 4
        wh_w = sb("wh_w", [P, K, H0, D])
        wa_w = sb("wa_w", [P, K, P])
        a0_b = sb("a0_b", [P, H0, 2 * D])
        wout_w = sb("wout_w", [P, KH, D + 2])
        aout_b = sb("aout_b", [P, 2 * D])
        w1_w = sb("w1_w", [P, K, D])
        w2_w = sb("w2_w", [P, K, D])
        b1_c = sb("b1_c", [P, K])
        b2_b = sb("b2_b", [P, D])
        gamma_b = sb("gamma_b", [P, D])
        beta_b = sb("beta_b", [P, D])
        wq_w = sb("wq_w", [P, K, D])
        wk_w = sb("wk_w", [P, K, D])
        wv_w = sb("wv_w", [P, K, D])
        wo_w = sb("wo_w", [P, K, D])
        bq_c = sb("bq_c", [P, K])
        bk_c = sb("bk_c", [P, K])
        bv_b = sb("bv_b", [P, D])
        bo_b = sb("bo_b", [P, D])
        wij_w = sb("wij_w", [P, K, 2 * D])
        bl2_b = sb("bl2_b", [P, D])
        w3_w = sb("w3_w", [P, K, F3 + 2])
        a3_b = sb("a3_b", [P, 2 * F3])
        deg_bl2 = sb("deg_bl2", [P, D])
        products = sb("products", [P, PRODUCTS, D])
        waited, pool_waited = sb("waited", [P, K]), sb("pool_waited", [P, 4])

        def high_low(name, shape):
            return sb(name + "_high", shape, F32R), sb(name + "_low", shape, F32R)

        wh_hl = high_low("wh", [P, K, H0, D])
        wout_hl = high_low("wout", [P, KH, D + 2])
        w2_hl = high_low("w2", [P, K, D])
        wv_hl = high_low("wv", [P, K, D])
        wo_hl = high_low("wo", [P, K, D])
        wij_hl = high_low("wij", [P, K, 2 * D])

        xs = sb("xs", [P, SLOTS, D])

        A_st, A_mv, A_ve, A_rs = sb("A_st", [P, 6]), sb("A_mv", [P, 2]), sb("A_ve", [P, 1]), sb("A_rs", [P, 1])
        A_z, A_hT = sb("A_z_t", [P, D]), sb("A_hT_t", [P, D])
        A_hl = high_low("A_hT", [P, D])
        A_f = sb("A_f_t", [P, 2 * H0])
        A_f3, A_frest = sb("A_f3", [P, P], BF16), sb("A_frest_t", [P, 2 * H0])
        A_f1T = sb("A_f1T", [P, P], BF16)
        A_f2T = sb("A_f2T", [P, H0, P], BF16)
        A_l = sb("A_l", [P, H0, P])
        A_m, A_sum, A_rec = sb("A_m", [P, H0]), sb("A_sum_t", [P, H0]), sb("A_rec", [P, H0])
        whs = sb("whs", [P, H0, D])
        attnT = sb("attnT", [P, H0, P])
        B_e = sb("B_e", [P, HD])
        B_hl = high_low("B_h", [P, HD])
        wh2 = sb("wh2", [P, D + 2])
        C_f3, C_frest, C_fT = sb("C_f3", [P, 3 * 2], BF16), sb("C_frest_t", [P, 2]), sb("C_fT_t", [P, P], BF16)
        C_l, C_aT = sb("C_l", [P, P]), sb("C_aT", [P, P])
        C_m, C_sum, C_rec = sb("C_m", [P, 1]), sb("C_sum", [P, 1]), sb("C_rec", [P, 1])
        C_e, C_h, C_hb, C_hT, C_hid = (sb(n, [P, D]) for n in ("C_e", "C_h_t", "C_hb_t", "C_hT_t", "C_hid_t"))
        C_hl = high_low("C_hid", [P, D])
        C_y, C_g = sb("C_y_t", [P, D]), sb("C_g_t", [P, D])
        C_st, C_mv, C_ve, C_rs = sb("C_st", [P, 6]), sb("C_mv", [P, 2]), sb("C_ve", [P, 1]), sb("C_rs", [P, 1])
        D_st, D_mv, D_ve, D_rs = sb("D_st", [P, 6]), sb("D_mv", [P, 2]), sb("D_ve", [P, 1]), sb("D_rs", [P, 1])
        D_z, D_hT = sb("D_z_t", [P, D]), sb("D_hT_t", [P, D])
        D_hl = high_low("D_hT", [P, D])
        D_q, D_k = sb("D_q_t", [P, D]), sb("D_k_t", [P, K, P])
        D_qhl = high_low("D_q", [P, D])
        D_khl = high_low("D_k", [P, K, HPC, P])
        D_v = sb("D_v_t", [P, HEADS_L1 + P // (DH + 1), DH + 1])
        F_s = sb("F_s_t", [P, HEADS_L1, P])
        F_pT = sb("F_pT_t", [P, HEADS_L1, P])
        F_m, F_rec = sb("F_m", [P, HEADS_L1]), sb("F_rec", [P, HEADS_L1])
        F_o = sb("F_o_t", [P, D])
        F_hl = high_low("F_oT", [P, D])
        E_st, E_mv, E_ve, E_rs = sb("E_st", [P, 6]), sb("E_mv", [P, 2]), sb("E_ve", [P, 1]), sb("E_rs", [P, 1])
        E_z, E_hT = sb("E_z_t", [P, D]), sb("E_hT_t", [P, D])
        E_hl = high_low("E_h", [P, D])
        E_ahl = high_low("E_ah", [P, 2 * D])
        E_h = sb("E_h_t", [P, F3 + 2])
        E_f3, E_frest, E_fT = sb("E_f3", [P, 3 * 2], BF16), sb("E_frest_t", [P, 2]), sb("E_fT_t", [P, P], BF16)
        E_l, E_aT = sb("E_l", [P, P]), sb("E_aT", [P, P])
        E_m, E_sum, E_rec = sb("E_m_t", [P, 1]), sb("E_sum", [P, 1]), sb("E_rec", [P, 1])

        pA = ps("pA", [P, 2, 512])
        pB = ps("pB", [P, 2, 512])
        pC = ps("pC", [P, 512])
        pF = ps("pF", [P, 2, 512])
        pE = ps("pE", [P, 512])

        S = {name: sem(name) for name in STEP_SEMAPHORES}
        first_loaded = sem("first_loaded")
        weights_loaded = sem("weights_loaded")
        highs_made = sem("highs_made")
        lows_made = sem("lows_made")
        consts_built = sem("consts_built")
        adj_ready = sem("adj_ready")
        adjT_done = sem("adjT_done")
        dve_setup = sem("dve_setup")
        x_loaded = sem("x_loaded")
        stored = sem("stored")

        def slot(g):
            return xs[:, g % SLOTS, :]

        def done(eng, name, g):
            eng.wait_ge(S[name], g + 1)

        def done_apart(eng, name, g):
            eng.wait_ge(consts_built, BUILT)
            done(eng, name, g)

        def done_before(eng, name, g):
            if not (isinstance(g, int) and g == 0):
                eng.wait_ge(S[name], g)

        def done_in_round(eng, name, chain, g, back=0):
            other = g + CHAINS.index(chain) - CHAINS.index(name[0]) - back
            if not isinstance(other, int) or 0 <= other < GRAPHS:
                done(eng, name, other)

        def rounds(eng, order, steps):
            def one(i):
                for name in order:
                    g = i - CHAINS.index(name[0])
                    if not isinstance(g, int) or 0 <= g < GRAPHS:
                        steps[name](g)
            turns = (GRAPHS - len(CHAINS)) // UNROLLED
            first = GRAPHS - turns * UNROLLED
            for i in range(first):
                one(i)
            with eng.Fori(first, GRAPHS, UNROLLED) as i:
                for k in range(UNROLLED):
                    one(i + k)
            for i in range(GRAPHS, GRAPHS + len(CHAINS) - 1):
                one(i)

        first_small_loads = [
            (a0_b[:, :, :].rearrange("p h d -> p (h d)"), a_heads.rearrange("h d -> (h d)").partition_broadcast(P)),
        ]
        small_loads = [
            (b1_c[:, :], b1),
            (bq_c[:, :], bq),
            (bk_c[:, :], bk),
            (b2_b[:, :], b2.partition_broadcast(P)),
            (gamma_b[:, :], gamma.partition_broadcast(P)),
            (beta_b[:, :], beta.partition_broadcast(P)),
            (bv_b[:, :], bv.partition_broadcast(P)),
            (bo_b[:, :], bo.partition_broadcast(P)),
            (bl2_b[:, :], b_l2.partition_broadcast(P)),
            (aout_b[:, :], a_out.partition_broadcast(P)),
            (a3_b[:, :], a_l3.rearrange("t f one -> (t f one)").partition_broadcast(P)),
        ]
        first_loads = [(wh_w[:, c, :, :], w_heads[:, c * P:(c + 1) * P, :].rearrange("h p d -> p h d"))
                       for c in range(K)]
        first_loads += [(adj_i[:, :], adj)]
        loads = [(wout_w[:, :, 0:D], w_out.rearrange("(k p) d -> p k d", p=P)),
                  (w3_w[:, :, 0:F3], w_l3.rearrange("(k p) d -> p k d", p=P))]
        loads += [(t[:, :, :], w.rearrange("(k p) d -> p k d", p=P))
                  for t, w in ((w1_w, w1), (w2_w, w2), (wq_w, wqT), (wk_w, wkT), (wv_w, wvT), (wo_w, woT), (wij_w, wijT))]
        ZEROED, BUILT = 14, 25
        DVE_SETUP = 8 + 2 * (K * H0 + KH + K)
        FIRST_LOADED = 16 * (len(first_loads) + len(first_small_loads))
        LOADED = 16 * (len(loads) + len(small_loads))
        pool_splits = [(w2_w, w2_hl), (wv_w, wv_hl), (wo_w, wo_hl), (wij_w, wij_hl)]
        dve_splits = [(wh_w, wh_hl), (wout_w, wout_hl)]
        LOWS_MADE = len(pool_splits) + len(dve_splits)

        def flat(t):
            return t[:, :, :, :].rearrange("p k h d -> p (k h d)") if len(t.shape) == 4 \
                else t[:, :, :].rearrange("p k d -> p (k d)")

        block = ctx.enter_context(nc.Block())

        @block.sync
        def _(sp):
            for dst, src in first_loads:
                sp.dma_start(dst, src).then_inc(first_loaded, 16)
            for dst, src in loads:
                sp.dma_start(dst, src).then_inc(weights_loaded, 16)

            def load(g, freed):
                if freed:
                    sp.wait_ge(stored, 16 * (g - SLOTS + 1))
                if not (isinstance(g, int) and g == 0):
                    sp.wait_ge(x_loaded, 16 * g)
                sp.dma_start(slot(g), x[g]).then_inc(x_loaded, 16)

            def store(g):
                done(sp, "E_left", g)
                done(sp, "E_right", g)
                sp.dma_start(out[g], slot(g)).then_inc(stored, 16)

            for g in range(SLOTS):
                load(g, freed=False)
            with sp.Fori(0, GRAPHS - SLOTS) as g:
                store(g)
                load(g + SLOTS, freed=True)
            for g in range(GRAPHS - SLOTS, GRAPHS):
                sp.wait_ge(stored, 16 * g)
                store(g)
            sp.wait_ge(stored, 16 * GRAPHS)

        @block.gpsimd
        def _(pool):
            pool.memset(ident[:, :], 0.0).then_inc(consts_built, 1)
            pool.memset(pick0[:, :, :], 0.0).then_inc(consts_built, 1)
            pool.memset(pick[:, :, :], 0.0).then_inc(consts_built, 1)
            for t in D_khl:
                pool.memset(t[:, :, :, :].bitcast(F32), 0.0).then_inc(consts_built, 1)
            pool.memset(minus_half[:, :], -0.5).then_inc(consts_built, 1)
            pool.memset(eps[:, :], EPS).then_inc(consts_built, 1)
            pool.memset(zeros[:, :], 0.0).then_inc(consts_built, 1)
            pool.memset(A_f3[:, :], 0.0).then_inc(consts_built, 1)
            for t in (A_f1T, C_fT, E_fT):
                pool.memset(t[:, :], 0.0).then_inc(consts_built, 1)
            pool.memset(wa_w[:, :, :], 0.0).then_inc(consts_built, 1)
            pool.memset(D_v[:, :, :], 1.0).then_inc(consts_built, 1)
            pool.wait_ge(consts_built, ZEROED)
            pool.affine_select(out=ident[:, :], in_=ident[:, :], compare_op=ALU.not_equal, fill=1.0, base=0,
                               pattern=[[-1, P]], channel_multiplier=1).then_inc(consts_built, 1)
            built = ZEROED + 1
            for t, logits, rows in ((pick0, H0, 0), (pick0, H0, HALF), (pick, 2, 0)):
                for part in range(3):
                    pool.affine_select(out=t[:, :, :], in_=t[:, :, :], compare_op=ALU.not_equal, fill=1.0,
                                       base=-rows - part * logits, pattern=[[-1, logits], [0, P]], channel_multiplier=1)\
                        .then_inc(consts_built, 1)
                    built += 1
                    pool.wait_ge(consts_built, built)
            pool.affine_select(out=A_f1T[:, :], in_=A_f1T[:, :], compare_op=ALU.is_ge, fill=1.0,
                               base=HALF - 1, pattern=[[0, P]], channel_multiplier=-1).then_inc(consts_built, 1)
            built += 1
            assert built == BUILT
            pool.wait_ge(weights_loaded, LOADED)
            for i, (w, (high, low)) in enumerate(pool_splits):
                pool.wait_ge(highs_made, 2 + i)
                pool.tensor_tensor(flat(low), flat(w), flat(high).bitcast(F32), ALU.subtract).then_inc(lows_made, 1)

            def rstd(chain, suffix, mv, ve, rs, nth=1, per_graph=1):
                def step(g):
                    done(pool, chain + "_moments" + suffix, g)
                    pool.tensor_tensor(ve[:, :], mv[:, 1:2], eps[:, :], ALU.add).then_inc(S[chain + "_var"], 1)
                    pool.wait_ge(S[chain + "_var"], per_graph * g + nth)
                    pool.tensor_tensor(rs[:, :], ve[:, :], minus_half[:, :], ALU.pow)\
                        .then_inc(S[chain + "_rstd" + suffix], 1)
                return step

            def split_in_three(chain, after, f, part, rest, zero):
                parts = S[chain + "_fparts"]

                def step(g):
                    done(pool, after, g)
                    pool.tensor_tensor(part(0), f, zero, ALU.add).then_inc(parts, 1)
                    pool.wait_ge(parts, 3 * g + 1)
                    pool.tensor_tensor(rest, f, part(0), ALU.subtract).then_inc(parts, 1)
                    pool.wait_ge(parts, 3 * g + 2)
                    pool.tensor_tensor(part(1), rest, zero, ALU.add).then_inc(parts, 1)
                    pool.wait_ge(parts, 3 * g + 3)
                    pool.tensor_tensor(part(2), rest, part(1), ALU.subtract).then_inc(S[chain + "_fcopy"], 1)
                return step

            def side_by_side(f3):
                return lambda k: f3[:, 2 * k:2 * (k + 1)]

            def halves(t):
                return t.rearrange("p (t h) -> p t h", t=2)

            def A_part(k):
                return halves(A_f3[:, 0:2 * HALF])[:, :, k * H0:(k + 1) * H0]

            def low_part(after, signal, hl, x, cols):
                def step(g):
                    done(pool, after, g)
                    pool.tensor_tensor(hl[1][:, cols], x[:, cols], hl[0][:, cols].bitcast(F32), ALU.subtract)\
                        .then_inc(S[signal], 1)
                return step

            def carry_waits(nth):
                pool.tensor_tensor(pool_waited[:, nth:nth + 1], eps[:, :], eps[:, :], ALU.add)

            def C_xb(g):
                done(pool, "A_z", g)
                carry_waits(0)
                pool.tensor_tensor(slot(g), slot(g), beta_b[:, :], ALU.add).then_inc(S["C_xb"], 1)

            def C_hb_step(g):
                done(pool, "C_h", g)
                pool.tensor_tensor(C_hb[:, :], C_h[:, :], b2_b[:, :], ALU.add).then_inc(S["C_hb"], 1)

            def D_xb(g):
                done(pool, "D_z", g)
                carry_waits(1)
                pool.tensor_tensor(slot(g), slot(g), bo_b[:, :], ALU.add).then_inc(S["D_xb"], 1)

            def E_xb(g):
                done(pool, "E_z", g)
                carry_waits(2)
                pool.tensor_tensor(slot(g), slot(g), deg_bl2[:, :], ALU.add).then_inc(S["E_xb"], 1)

            def E_right(g):
                done(pool, "E_hc", g)
                done(pool, "E_z3", g)
                carry_waits(3)
                right = xs[:, g % SLOTS, F3:D]
                pool.tensor_tensor(right, right, E_h[:, 0:F3], ALU.add).then_inc(S["E_right"], 1)

            rounds(pool, POOL_ORDER, {
                "A_rstd": rstd("A", "", A_mv, A_ve, A_rs), "C_rstd": rstd("C", "", C_mv, C_ve, C_rs),
                "D_rstd": rstd("D", "", D_mv, D_ve, D_rs), "E_rstd": rstd("E", "", E_mv, E_ve, E_rs, 1, 2),
                "E_rstd3": rstd("E", "3", E_mv, E_ve, E_rs, 2, 2),
                "A_fcopy": split_in_three("A", "A_fc", halves(A_f[:, :]), A_part,
                                          halves(A_frest[:, :]), halves(zeros[:, :])),
                "C_fcopy": split_in_three("C", "B_whc", wh2[:, D:D + 2], side_by_side(C_f3), C_frest[:, :],
                                          zeros[:, 0:2]),
                "E_fcopy": split_in_three("E", "E_hc", E_h[:, F3:F3 + 2], side_by_side(E_f3), E_frest[:, :],
                                          zeros[:, 0:2]),
                "A_low": low_part("A_high", "A_low", A_hl, A_hT, slice(0, D)),
                "B_low": low_part("B_high", "B_low", B_hl, B_e, slice(HD // 2, HD)),
                "C_low": low_part("C_high", "C_low", C_hl, C_hid, slice(0, D)),
                "D_low": low_part("D_high", "D_low", D_hl, D_hT, slice(0, D)),
                "D_qlow": low_part("D_qhigh", "D_qlow", D_qhl, D_q, slice(0, D)),
                "C_xb": C_xb, "C_hb": C_hb_step, "D_xb": D_xb, "E_xb": E_xb, "E_right": E_right,
            })

        @block.scalar
        def _(act):
            for dst, src in first_small_loads:
                act.dma_start(dst, src).then_inc(first_loaded, 16)
            for dst, src in small_loads:
                act.dma_start(dst, src).then_inc(weights_loaded, 16)
            act.wait_ge(first_loaded, FIRST_LOADED)
            act.activation(flat(wh_hl[0]), flat(wh_w), ACT.Copy).then_inc(highs_made, 1)
            act.wait_ge(weights_loaded, LOADED)
            for w, (high, low) in pool_splits:
                act.activation(flat(high), flat(w), ACT.Copy).then_inc(highs_made, 1)
            act.wait_ge(dve_setup, DVE_SETUP)
            act.activation(flat(wout_hl[0]), flat(wout_w), ACT.Copy).then_inc(highs_made, 1)

            def relu_copy(after, signal, dst, src):
                def step(g):
                    done(act, after, g)
                    act.activation(dst, src, ACT.Relu).then_inc(S[signal], 1)
                return step

            def copy(after, signal, dst, src):
                def step(g):
                    done(act, after, g)
                    act.activation(dst, src, ACT.Copy).then_inc(S[signal], 1)
                return step

            def A_whc_hi(g):
                done(act, "A_wh_hi", g)
                done_before(act, "B_o", g)
                act.activation(whs[:, 2:4, :].rearrange("p h d -> p (h d)"), pA[:, 1, :], ACT.Copy).then_inc(S["A_whc_hi"], 1)

            def A_whc_lo(g):
                done(act, "A_wh_lo", g)
                act.activation(whs[:, 0:2, :].rearrange("p h d -> p (h d)"), pA[:, 0, :], ACT.Copy).then_inc(S["A_whc_lo"], 1)

            def A_slope(g):
                done(act, "A_s", g)
                act.activation(A_l[:, :, :].rearrange("p h m -> p (h m)"), pA[:, 0, :], ACT.Copy, scale=SLOPE_L0)\
                   .then_inc(S["A_slope"], 1)

            def A_exp(g):
                done(act, "A_max", g)
                for h in range(H0):
                    last = act.activation(A_l[:, h, :], A_l[:, h, :], ACT.Exp, scale=-1.0, bias=A_m[:, h:h + 1],
                                          accum_out=A_sum[:, h:h + 1])
                last.then_inc(S["A_exp"], 1)

            def A_attn(g):
                done(act, "A_pT", g)
                done_before(act, "B_o", g)
                act.activation(attnT[:, :, :].rearrange("p h m -> p (h m)"), pA[:, 1, :], ACT.Copy).then_inc(S["A_attn"], 1)

            def half(t, c):
                return t[:, c * HD // 2:(c + 1) * HD // 2]

            def name_of(step, c):
                return step if c == 1 else step + "0"

            def B_neg(c):
                def step(g):
                    done(act, name_of("B_o", c), g)
                    act.activation(half(B_e, c), pB[:, c, :], ACT.Relu, scale=-1.0).then_inc(S[name_of("B_neg", c)], 1)
                return step

            def B_exp(c):
                def step(g):
                    done(act, name_of("B_neg", c), g)
                    act.activation(half(B_e, c), half(B_e, c), ACT.Exp, scale=-1.0).then_inc(S[name_of("B_exp", c)], 1)
                return step

            def B_high(c):
                def step(g):
                    done(act, name_of("B_h", c), g)
                    act.activation(half(B_hl[0], c), half(B_e, c), ACT.Copy).then_inc(S[name_of("B_high", c)], 1)
                return step

            def B_whc(g):
                done(act, "B_wh", g)
                done_before(act, "C_o", g)
                act.activation(wh2[:, :], pB[:, 0, 0:D + 2], ACT.Copy).then_inc(S["B_whc"], 1)

            def slope(chain, dst, src, alpha):
                def step(g):
                    done(act, chain + "_s", g)
                    act.activation(dst, src, ACT.Copy, scale=alpha).then_inc(S[chain + "_slope"], 1)
                return step

            def exp_and_sum(chain, t, minus_max, total):
                def step(g):
                    done(act, chain + "_max", g)
                    act.activation(t[:, :], t[:, :], ACT.Exp, scale=-1.0, bias=minus_max[:, :], accum_out=total[:, :])\
                       .then_inc(S[chain + "_exp"], 1)
                return step

            def C_oexp(g):
                done(act, "C_o", g)
                done(act, "C_recip", g)
                act.activation(C_e[:, :], pC[:, 0:D], ACT.Exp, scale=C_rec[:, :]).then_inc(S["C_oexp"], 1)

            def C_hidc(g):
                done(act, "C_hid", g)
                act.activation(C_hid[:, 0:P], pC[:, 0:P], ACT.Relu, bias=b1_c[:, 0:1])
                act.activation(C_hid[:, P:D], pC[:, P:D], ACT.Relu, bias=b1_c[:, 1:2]).then_inc(S["C_hidc"], 1)

            def D_kc(g):
                done(act, "D_kv", g)
                done_before(act, "D_klow", g)
                for c in range(K):
                    last = act.activation(D_k[:, c, :], pB[:, 1, c * P:(c + 1) * P], ACT.Identity, bias=bk_c[:, c:c + 1])
                last.then_inc(S["D_kc"], 1)

            def D_qc(g):
                done(act, "D_q", g)
                done_before(act, "D_qlow", g)
                for c in range(K):
                    last = act.activation(D_q[:, c * P:(c + 1) * P], pB[:, 1, c * P:(c + 1) * P], ACT.Identity,
                                          bias=bq_c[:, c:c + 1], scale=SCALE)
                last.then_inc(S["D_qc"], 1)

            def D_qhigh(g):
                done(act, "D_qc", g)
                done_before(act, "F_s", g)
                act.activation(D_qhl[0][:, :], D_q[:, :], ACT.Copy).then_inc(S["D_qhigh"], 1)

            def F_exp(c):
                def step(g):
                    done(act, "F_max" if c == K - 1 else "F_max0", g)
                    for h in range(c * HPC, (c + 1) * HPC):
                        last = act.activation(F_s[:, h, :], F_s[:, h, :], ACT.Exp, scale=-1.0, bias=F_m[:, h:h + 1])
                    last.then_inc(S["F_exp" if c == K - 1 else "F_exp0"], 1)
                return step

            def E_hc(g):
                done(act, "E_h", g)
                done_before(act, "E_right", g)
                act.activation(E_h[:, :], pE[:, 0:F3 + 2], ACT.Copy).then_inc(S["E_hc"], 1)

            rounds(act, ACT_ORDER, {
                "A_hT": relu_copy("A_zT", "A_hT", A_hT[:, :], pA[:, 0, 0:D]),
                "A_whc_hi": A_whc_hi, "A_whc_lo": A_whc_lo, "A_slope": A_slope, "A_exp": A_exp, "A_attn": A_attn,
                "A_fc": copy("A_f", "A_fc", A_f[:, :], pA[:, 0, 0:2 * H0]),
                "A_high": copy("A_hT", "A_high", A_hl[0][:, :], A_hT[:, :]),
                "B_neg.0": B_neg(0), "B_neg": B_neg(1), "B_exp.0": B_exp(0), "B_exp": B_exp(1),
                "B_high.0": B_high(0), "B_high": B_high(1), "B_whc": B_whc,
                "C_slope": slope("C", C_l[:, :], pC[:, 0:P], SLOPE_L0),
                "C_exp": exp_and_sum("C", C_l, C_m, C_sum),
                "C_attn": copy("C_pT", "C_attn", C_aT[:, :], pC[:, P:2 * P]),
                "C_oexp": C_oexp,
                "C_hTc": copy("C_hT", "C_hTc", C_hT[:, :], pC[:, D:2 * D]),
                "C_hidc": C_hidc, "C_high": copy("C_hidc", "C_high", C_hl[0][:, :], C_hid[:, :]),
                "D_hT": relu_copy("D_zT", "D_hT", D_hT[:, :], pB[:, 1, 0:D]),
                "D_high": copy("D_hT", "D_high", D_hl[0][:, :], D_hT[:, :]),
                "D_kc": D_kc, "D_qc": D_qc, "D_qhigh": D_qhigh, "F_exp.0": F_exp(0), "F_exp": F_exp(1),
                "F_pTc.0": copy("F_pT0", "F_pTc0", F_pT[:, 0:HPC, :].rearrange("p h n -> p (h n)"), pF[:, 0, :]),
                "F_pTc": copy("F_pT", "F_pTc", F_pT[:, HPC:2 * HPC, :].rearrange("p h n -> p (h n)"), pF[:, 1, :]),
                "F_high": copy("F_oT", "F_high", F_hl[0][:, :], pF[:, 1, 0:D]),
                "E_high": relu_copy("E_z", "E_high", E_hl[0][:, :], E_z[:, :]),
                "E_ahhigh": copy("E_ah", "E_ahhigh", E_ahl[0][:, :], pE[:, :]),
                "E_hT3": relu_copy("E_zT3", "E_hT3", E_hT[:, :], pE[:, D:2 * D]),
                "E_hc": E_hc,
                "E_slope": slope("E", E_l[:, :], pE[:, 384:512], SLOPE_L3),
                "E_exp": exp_and_sum("E", E_l, E_m, E_sum),
                "E_attn": copy("E_pT", "E_attn", E_aT[:, :], pE[:, 256:384]),
            })

        @block.vector
        def _(dve):
            dve.wait_ge(first_loaded, FIRST_LOADED)
            dve.wait_ge(consts_built, BUILT)
            dve.tensor_copy(adj_f[:, :], adj_i[:, :]).then_inc(adj_ready, 1)
            dve.wait_ge(adj_ready, 1)
            dve.tensor_reduce(deg[:, :], adj_f[:, :], AX.X, ALU.add).then_inc(dve_setup, 1)
            dve.tensor_scalar(mask[:, :], adj_f[:, :], 0.0, -1.0, ALU.is_gt, ALU.add).then_inc(adj_ready, 1)
            dve.wait_ge(adj_ready, 2)
            dve.tensor_scalar(mask[:, :], mask[:, :], -MASKED, None, ALU.mult).then_inc(dve_setup, 1)
            dve.tensor_copy(ident_bf[:, :], ident[:, :]).then_inc(dve_setup, 1)
            dve.wait_ge(dve_setup, 3)
            dve.tensor_scalar(adj_deg[:, P:2 * P], ident[:, :], deg[:, 0:1], None, ALU.mult).then_inc(dve_setup, 1)
            dve.wait_ge(adjT_done, 1)
            dve.tensor_copy(adj_deg[:, 0:P], pA[:, 0, 0:P]).then_inc(dve_setup, 1)
            dve.tensor_copy(A_f2T[:, :, :], pick0[:, :, :]).then_inc(dve_setup, 1)
            count = 6
            dots = [(wh_w[:, c, h, :], a0_b[:, h, t * D:(t + 1) * D], wa_w[:, c, t * H0 + h:t * H0 + h + 1])
                    for c in range(K) for h in range(H0) for t in range(2)]
            first_dots = len(dots)
            dots += [(wout_w[:, c, 0:D], aout_b[:, t * D:(t + 1) * D], wout_w[:, c, D + t:D + t + 1])
                     for c in range(KH) for t in range(2)]
            dots += [(w3_w[:, c, 0:F3], a3_b[:, t * F3:(t + 1) * F3], w3_w[:, c, F3 + t:F3 + t + 1])
                     for c in range(K) for t in range(2)]
            for i, (w, a, dot) in enumerate(dots):
                if i == first_dots:
                    dve.wait_ge(weights_loaded, LOADED)
                if i >= PRODUCTS:
                    dve.wait_ge(dve_setup, count - PRODUCTS + 1)
                dve.tensor_tensor_reduce(products[:, i % PRODUCTS, 0:a.shape[1]], w, a, 1.0, 0.0, ALU.mult, ALU.add, dot)\
                   .then_inc(dve_setup, 1)
                count += 1
            dve.tensor_scalar(bq_c[:, :], bq_c[:, :], SCALE, None, ALU.mult).then_inc(dve_setup, 1)
            dve.tensor_scalar(deg_bl2[:, :], bl2_b[:, :], deg[:, 0:1], None, ALU.mult).then_inc(dve_setup, 1)
            assert count + 2 == DVE_SETUP
            for (w, (high, low)), made in zip(dve_splits, (1, LOWS_MADE)):
                dve.wait_ge(highs_made, made)
                dve.tensor_tensor(flat(low), flat(w), flat(high).bitcast(F32), ALU.subtract).then_inc(lows_made, 1)

            def stats(chain, suffix, x, st, after):
                def step(g):
                    if x is slot:
                        dve.wait_ge(consts_built, BUILT)
                    after(g)
                    dve.bn_stats(st[:, :], x(g)).then_inc(S[chain + "_stats" + suffix], 1)
                return step

            def moments(chain, suffix, st, mv):
                def step(g):
                    done_apart(dve, chain + "_stats" + suffix, g)
                    dve.bn_aggr(mv[:, :], st[:, :]).then_inc(S[chain + "_moments" + suffix], 1)
                return step

            def normalise(chain, suffix, z, mv, rs):
                def step(g):
                    done(dve, chain + "_rstd" + suffix, g)
                    dve.tensor_scalar(z[:, :], slot(g), mv[:, 0:1], rs[:, 0:1], ALU.subtract, ALU.mult)\
                       .then_inc(S[chain + "_z" + suffix], 1)
                return step

            def copy(after, signal, dst, src):
                def step(g):
                    done(dve, after, g)
                    dve.tensor_copy(dst, src).then_inc(S[signal], 1)
                return step

            def low_part(after, signal, hl, x, cols):
                def step(g):
                    done(dve, after, g)
                    dve.tensor_tensor(hl[1][:, cols], x[:, cols], hl[0][:, cols].bitcast(F32), ALU.subtract)\
                       .then_inc(S[signal], 1)
                return step

            def A_fTc(g):
                done(dve, "A_fT", g)
                dve.tensor_copy(A_f1T[0:HALF, :], pA[0:HALF, 1, 0:P // 2].bitcast(BF16))
                f2 = pA[HALF:2 * HALF, 1, 0:P // 2].bitcast(BF16).unsqueeze(1).to_broadcast([HALF, H0, P])
                dve.tensor_tensor(A_f2T[HALF:2 * HALF, :, :], f2, pick0[HALF:2 * HALF, :, :], ALU.mult)\
                   .then_inc(S["A_fTc"], 1)

            def A_leaky(g):
                done(dve, "A_slope", g)
                flat = A_l[:, :, :].rearrange("p h m -> p (h m)")
                dve.tensor_tensor(flat, pA[:, 0, :], flat, ALU.max).then_inc(S["A_leaky"], 1)

            def mask_and_max(dst, scores, minus_max):
                return dve.tensor_tensor_reduce(dst, scores, mask[:, :], -1.0, HUGE, ALU.add, ALU.min, minus_max)

            def A_max(g):
                done_apart(dve, "A_leaky", g)
                for h in range(H0):
                    last = mask_and_max(A_l[:, h, :], A_l[:, h, :], A_m[:, h:h + 1])
                last.then_inc(S["A_max"], 1)

            def A_norm(g):
                done(dve, "A_recip", g)
                dve.tensor_tensor(A_l[:, :, :], A_l[:, :, :], A_rec[:, :].unsqueeze(2).to_broadcast([P, H0, P]), ALU.mult)\
                   .then_inc(S["A_norm"], 1)

            def B_h(c):
                def step(g):
                    done(dve, "B_exp" if c == 1 else "B_exp0", g)
                    e = B_e[:, c * HD // 2:(c + 1) * HD // 2]
                    dve.scalar_tensor_tensor(out=e, in0=e, scalar=-1.0, in1=pB[:, c, :], op0=ALU.add, op1=ALU.max)\
                       .then_inc(S["B_h" if c == 1 else "B_h0"], 1)
                return step

            def leaky(chain, t, scores):
                def step(g):
                    done(dve, chain + "_slope", g)
                    dve.tensor_tensor(t[:, :], scores, t[:, :], ALU.max).then_inc(S[chain + "_leaky"], 1)
                return step

            def minus_max(chain, m, t):
                def step(g):
                    done_apart(dve, chain + "_leaky", g)
                    mask_and_max(t[:, :], t[:, :], m[:, :]).then_inc(S[chain + "_max"], 1)
                return step

            def recip(chain, r, total):
                def step(g):
                    done(dve, chain + "_exp", g)
                    dve.reciprocal(r[:, :], total[:, :]).then_inc(S[chain + "_recip"], 1)
                return step

            def C_min(g):
                done(dve, "C_oexp", g)
                dve.tensor_scalar(C_e[:, :], C_e[:, :], 1.0, -1.0, ALU.min, ALU.add).then_inc(S["C_min"], 1)

            def C_h_step(g):
                done(dve, "C_min", g)
                done_before(dve, "C_hb", g)
                dve.scalar_tensor_tensor(out=C_h[:, :], in0=pC[:, 0:D], scalar=C_rec[:, :], in1=C_e[:, :],
                                         op0=ALU.mult, op1=ALU.max).then_inc(S["C_h"], 1)

            def C_y_step(g):
                done(dve, "C_ffn", g)
                done(dve, "C_hb", g)
                dve.tensor_tensor(C_y[:, :], pC[:, D:2 * D], C_hb[:, :], ALU.add).then_inc(S["C_y"], 1)

            def C_g_step(g):
                done(dve, "C_moments", g)
                dve.scalar_tensor_tensor(out=C_g[:, :], in0=C_y[:, :], scalar=C_mv[:, 0:1], in1=gamma_b[:, :],
                                         op0=ALU.subtract, op1=ALU.mult).then_inc(S["C_g"], 1)

            def C_x1(g):
                done(dve, "C_g", g)
                done(dve, "C_rstd", g)
                done(dve, "C_xb", g)
                dve.scalar_tensor_tensor(out=slot(g), in0=C_g[:, :], scalar=C_rs[:, 0:1], in1=slot(g),
                                         op0=ALU.mult, op1=ALU.add).then_inc(S["C_x1"], 1)

            def own_block(t, h):
                return t[h * DH:(h + 1) * DH, :, h, :]

            def D_khigh(g):
                done(dve, "D_kc", g)
                done_before(dve, "F_s", g)
                for h in range(HPC):
                    last = dve.tensor_copy(own_block(D_khl[0], h), D_k[h * DH:(h + 1) * DH, :, :])
                last.then_inc(S["D_khigh"], 1)

            def D_klow(g):
                done(dve, "D_khigh", g)
                for h in range(HPC):
                    last = dve.tensor_tensor(own_block(D_khl[1], h), D_k[h * DH:(h + 1) * DH, :, :],
                                             own_block(D_khl[0], h).bitcast(F32), ALU.subtract)
                last.then_inc(S["D_klow"], 1)

            def D_vc(g):
                done(dve, "D_kc", g)
                done_before(dve, "F_o", g)
                heads = lambda t: t.rearrange("p (h d) -> p h d", h=HEADS_L1)
                dve.tensor_tensor(D_v[:, 0:HEADS_L1, 0:DH], heads(pB[:, 1, D:2 * D]), heads(bv_b[:, :]), ALU.add)\
                   .then_inc(S["D_vc"], 1)

            def F_max(c):
                def step(g):
                    done(dve, "F_s" if c == K - 1 else "F_s0", g)
                    dve.memset(waited[:, c:c + 1], 0.0)
                    for h in range(c * HPC, (c + 1) * HPC):
                        last = mask_and_max(F_s[:, h, :], pF[:, c, (h % HPC) * P:(h % HPC + 1) * P], F_m[:, h:h + 1])
                    last.then_inc(S["F_max" if c == K - 1 else "F_max0"], 1)
                return step

            def F_recip(g):
                done(dve, "F_o", g)
                o = pF[:, :, :].rearrange("p b (h d) -> p (b h) d", d=P)
                dve.reciprocal(F_rec[:, :].unsqueeze(2), o[:, :, DH:DH + 1]).then_inc(S["F_recip"], 1)

            def F_on(g):
                done(dve, "F_recip", g)
                o = pF[:, :, :].rearrange("p b (h d) -> p (b h) d", d=P)
                dve.tensor_tensor(F_o[:, :].rearrange("p (h d) -> p h d", h=HEADS_L1), o[:, :, 0:DH],
                                  F_rec[:, :].unsqueeze(2).to_broadcast([P, HEADS_L1, DH]), ALU.mult)\
                   .then_inc(S["F_on"], 1)

            def F_x2(g):
                done(dve, "F_out", g)
                done(dve, "D_xb", g)
                dve.tensor_tensor(slot(g), pF[:, 1, D:2 * D], slot(g), ALU.add).then_inc(S["F_x2"], 1)

            def E_low_step(g):
                done(dve, "E_high", g)
                dve.scalar_tensor_tensor(out=E_hl[1][:, :], in0=E_z[:, :], scalar=0.0, in1=E_hl[0][:, :].bitcast(F32),
                                         op0=ALU.max, op1=ALU.subtract).then_inc(S["E_low"], 1)

            def E_x3(g):
                done(dve, "E_m", g)
                done(dve, "E_xb", g)
                dve.tensor_tensor(slot(g), pE[:, 0:D], slot(g), ALU.add).then_inc(S["E_x3"], 1)

            def E_left(g):
                done(dve, "E_o", g)
                done(dve, "E_recip", g)
                left = xs[:, g % SLOTS, 0:F3]
                dve.scalar_tensor_tensor(out=left, in0=pE[:, 384:512], scalar=E_rec[:, :], in1=left,
                                         op0=ALU.mult, op1=ALU.add).then_inc(S["E_left"], 1)

            rounds(dve, DVE_ORDER, {
                "A_stats": stats("A", "", slot, A_st, lambda g: dve.wait_ge(x_loaded, 16 * (g + 1))),
                "A_moments": moments("A", "", A_st, A_mv), "A_z": normalise("A", "", A_z, A_mv, A_rs),
                "A_fTc": A_fTc,
                "A_leaky": A_leaky, "A_max": A_max, "A_recip": recip("A", A_rec, A_sum), "A_norm": A_norm,
                "B_h.0": B_h(0), "B_h": B_h(1), "B_low.0": low_part("B_high0", "B_low0", B_hl, B_e, slice(0, HD // 2)),
                "C_fTc": copy("C_fT", "C_fTc", C_fT[0:6, :], pC[0:6, D:D + P // 2].bitcast(BF16)),
                "C_leaky": leaky("C", C_l, pC[:, 0:P]), "C_max": minus_max("C", C_m, C_l),
                "C_recip": recip("C", C_rec, C_sum), "C_min": C_min, "C_h": C_h_step, "C_y": C_y_step,
                "C_stats": stats("C", "", lambda g: C_y[:, :], C_st, lambda g: done(dve, "C_y", g)),
                "C_moments": moments("C", "", C_st, C_mv), "C_g": C_g_step, "C_x1": C_x1,
                "D_stats": stats("D", "", slot, D_st, lambda g: done(dve, "C_x1", g)),
                "D_moments": moments("D", "", D_st, D_mv), "D_z": normalise("D", "", D_z, D_mv, D_rs),
                "D_khigh": D_khigh, "D_klow": D_klow, "D_vc": D_vc, "F_max.0": F_max(0),
                "F_max": F_max(1), "F_recip": F_recip, "F_on": F_on,
                "F_low": low_part("F_high", "F_low", F_hl, pF[:, 1, :], slice(0, D)), "F_x2": F_x2,
                "E_stats": stats("E", "", slot, E_st, lambda g: done(dve, "F_x2", g)),
                "E_moments": moments("E", "", E_st, E_mv), "E_z": normalise("E", "", E_z, E_mv, E_rs),
                "E_low": E_low_step, "E_ahlow": low_part("E_ahhigh", "E_ahlow", E_ahl, pE, slice(0, 2 * D)),
                "E_x3": E_x3,
                "E_stats3": stats("E", "3", slot, E_st, lambda g: done(dve, "E_x3", g)),
                "E_moments3": moments("E", "3", E_st, E_mv), "E_z3": normalise("E", "3", E_z, E_mv, E_rs),
                "E_fTc": copy("E_fT", "E_fTc", E_fT[0:6, :], pE[0:6, 256:256 + P // 2].bitcast(BF16)),
                "E_leaky": leaky("E", E_l, pE[:, 384:512]), "E_max": minus_max("E", E_m, E_l),
                "E_recip": recip("E", E_rec, E_sum), "E_left": E_left,
            })

        @block.tensor
        def _(pe):
            pe.wait_ge(consts_built, BUILT)
            pe.wait_ge(adj_ready, 1)
            pe.transpose(pA[:, 0, 0:P], adj_f[:, :], ident[:, :]).then_inc(adjT_done, 1)
            pe.wait_ge(weights_loaded, LOADED)
            pe.wait_ge(dve_setup, DVE_SETUP)
            pe.wait_ge(lows_made, LOWS_MADE)

            def transposes(dst, src, n):
                for j in range(n):
                    last = pe.transpose(dst[:, j * P:(j + 1) * P], src[:, j * P:(j + 1) * P], ident[:, :])
                return last

            def project(dst, hT, w):
                for k in range(K):
                    last = pe.matmul(dst, hT[:, k * P:(k + 1) * P], w[:, k, :], start=(k == 0), stop=(k == K - 1))
                return last

            def split_product(dst, parts):
                terms = []
                for a_high, a_low, b_high, b_low in parts:
                    terms += [(a_high, b_high), (a_high, b_low), (a_low, b_high)]
                for i, (a, b) in enumerate(terms):
                    last = pe.matmul(dst, a, b, start=(i == 0), stop=(i == len(terms) - 1))
                return last

            def split_project(dst, hl, w_hl):
                return split_product(dst, [(hl[0][:, k * P:(k + 1) * P], hl[1][:, k * P:(k + 1) * P],
                                            w_hl[0][:, k, :], w_hl[1][:, k, :]) for k in range(K)])

            def A_zT(g):
                done(pe, "A_z", g)
                done_before(pe, "A_attn", g)
                transposes(pA[:, 0, :], A_z, K).then_inc(S["A_zT"], 1)

            def A_f(g):
                done(pe, "A_hT", g)
                project(pA[:, 0, 0:P], A_hT, wa_w).then_inc(S["A_f"], 1)

            def A_wh_hi(g):
                done(pe, "A_low", g)
                wh = [w[:, :, 2:4, :].rearrange("p k h d -> p k (h d)") for w in wh_hl]
                split_project(pA[:, 1, :], A_hl, wh).then_inc(S["A_wh_hi"], 1)

            def A_wh_lo(g):
                done(pe, "A_fc", g)
                wh = [w[:, :, 0:2, :].rearrange("p k h d -> p k (h d)") for w in wh_hl]
                split_project(pA[:, 0, :], A_hl, wh).then_inc(S["A_wh_lo"], 1)

            def logits_transposed(dst, f3):
                n = f3.shape[1]
                return pe.transpose(dst[0:n, 0:P // 2].bitcast(BF16), f3[:, :], ident_bf[:, :])

            def A_fT_step(g):
                done(pe, "A_fcopy", g)
                done(pe, "A_whc_hi", g)
                logits_transposed(pA[:, 1, :], A_f3).then_inc(S["A_fT"], 1)

            def A_s(g):
                done(pe, "A_fTc", g)
                done(pe, "A_whc_lo", g)
                pe.matmul(pA[:, 0, :], A_f1T[:, :], A_f2T[:, :, :].rearrange("r h m -> r (h m)"), start=True, stop=True)\
                    .then_inc(S["A_s"], 1)

            def A_pT(g):
                done(pe, "A_norm", g)
                transposes(pA[:, 1, :], A_l[:, :, :].rearrange("p h m -> p (h m)"), H0).then_inc(S["A_pT"], 1)

            def B_o(bank):
                def step(g):
                    if bank == 0:
                        done(pe, "A_attn", g)
                        done_before(pe, "B_whc", g)
                    else:
                        done_in_round(pe, "D_qc", "B", g, 1)
                    for k in range(bank * KH // 2, (bank + 1) * KH // 2):
                        h, c = k // K, k % K
                        last = pe.matmul(pB[:, bank, (k % 4) * P:(k % 4 + 1) * P], whs[:, h, c * P:(c + 1) * P],
                                         attnT[:, h, :], start=True, stop=True)
                    last.then_inc(S["B_o" if bank == 1 else "B_o0"], 1)
                return step

            def B_wh(part):
                def step(g):
                    if part == 0:
                        done(pe, "B_low0", g)
                    if part == 2:
                        done(pe, "B_low", g)
                    for k in range(part * KH // 4, (part + 1) * KH // 4):
                        high, low = (t[:, k * P:(k + 1) * P] for t in B_hl)
                        for i, (a, w) in enumerate(((high, wout_hl[0]), (high, wout_hl[1]), (low, wout_hl[0]))):
                            last = pe.matmul(pB[:, 0, 0:D + 2], a, w[:, k, :],
                                             start=(k == 0 and i == 0), stop=(k == KH - 1 and i == 2))
                    if part == 3:
                        last.then_inc(S["B_wh"], 1)
                return step

            def C_fT_step(g):
                done(pe, "C_fcopy", g)
                done_before(pe, "C_y", g)
                logits_transposed(pC[:, D:2 * D], C_f3).then_inc(S["C_fT"], 1)

            def one_head(dst, fT, signal):
                pe.matmul(dst, fT[:, :], pick[:, 0, :], start=True, stop=False)
                pe.matmul(dst, pick[:, 1, :], fT[:, :], start=False, stop=True).then_inc(S[signal], 1)

            def C_s(g):
                done(pe, "C_fTc", g)
                one_head(pC[:, 0:P], C_fT, "C_s")

            def C_pT(g):
                done(pe, "C_exp", g)
                pe.transpose(pC[:, P:2 * P], C_l[:, :], ident[:, :]).then_inc(S["C_pT"], 1)

            def C_o(g):
                done(pe, "C_attn", g)
                pe.matmul(pC[:, 0:D], C_aT[:, :], wh2[:, 0:D], start=True, stop=True).then_inc(S["C_o"], 1)

            def C_hT_step(g):
                done(pe, "C_h", g)
                transposes(pC[:, D:2 * D], C_h, K).then_inc(S["C_hT"], 1)

            def transposed_product(dst, w, hT):
                for c in range(K):
                    for k in range(K):
                        last = pe.matmul(dst[:, c * P:(c + 1) * P], w[:, k, c * P:(c + 1) * P], hT[:, k * P:(k + 1) * P],
                                         start=(k == 0), stop=(k == K - 1))
                return last

            def C_hid_step(g):
                done(pe, "C_hTc", g)
                transposed_product(pC[:, 0:D], w1_w, C_hT).then_inc(S["C_hid"], 1)

            def C_ffn(g):
                done(pe, "C_low", g)
                split_project(pC[:, D:2 * D], C_hl, w2_hl).then_inc(S["C_ffn"], 1)

            def D_zT(g):
                done(pe, "D_z", g)
                done_in_round(pe, "B_h", "D", g)
                transposes(pB[:, 1, :], D_z, K).then_inc(S["D_zT"], 1)

            def D_q_step(g):
                done(pe, "D_vc", g)
                transposed_product(pB[:, 1, 0:D], wq_w, D_hT).then_inc(S["D_q"], 1)

            def D_k_step(g):
                done(pe, "D_hT", g)
                transposed_product(pB[:, 1, 0:D], wk_w, D_hT)

            def D_v_step(g):
                done(pe, "D_low", g)
                split_project(pB[:, 1, D:2 * D], D_hl, wv_hl).then_inc(S["D_kv"], 1)

            def F_s_step(c):
                def step(g):
                    if c == 0:
                        done(pe, "D_klow", g)
                        done(pe, "D_qlow", g)
                        done_before(pe, "F_x2", g)
                    q_high, q_low = (t[:, c * P:(c + 1) * P] for t in D_qhl)
                    k_high, k_low = (t[:, c, :, :].rearrange("p h m -> p (h m)") for t in D_khl)
                    last = split_product(pF[:, c, :], [(q_high, q_low, k_high, k_low)])
                    last.then_inc(S["F_s" if c == K - 1 else "F_s0"], 1)
                return step

            def F_pT_step(c):
                def step(g):
                    done(pe, "F_exp" if c == K - 1 else "F_exp0", g)
                    heads = F_s[:, c * HPC:(c + 1) * HPC, :].rearrange("p h m -> p (h m)")
                    transposes(pF[:, c, :], heads, HPC).then_inc(S["F_pT" if c == K - 1 else "F_pT0"], 1)
                return step

            def F_o_step(c):
                def step(g):
                    done(pe, "F_pTc" if c == K - 1 else "F_pTc0", g)
                    v = D_v[:, :, :].rearrange("p h d -> p (h d)")
                    for h in range(c * HPC, (c + 1) * HPC):
                        last = pe.matmul(pF[:, c, (h % HPC) * P:(h % HPC + 1) * P], F_pT[:, h, :],
                                         v[:, h * (DH + 1):h * (DH + 1) + P], start=True, stop=True)
                    if c == K - 1:
                        last.then_inc(S["F_o"], 1)
                return step

            def F_oT_step(g):
                done(pe, "F_on", g)
                transposes(pF[:, 1, :], F_o, K).then_inc(S["F_oT"], 1)

            def F_out(g):
                done(pe, "F_low", g)
                split_project(pF[:, 1, D:2 * D], F_hl, wo_hl).then_inc(S["F_out"], 1)

            def E_ah(g):
                done(pe, "E_low", g)
                for c in range(K):
                    for i, h in enumerate(E_hl):
                        last = pe.matmul(pE[:, c * D:(c + 1) * D], h[:, c * P:(c + 1) * P], adj_deg[:, :],
                                         start=(i == 0), stop=(i == 1))
                last.then_inc(S["E_ah"], 1)

            def E_m(g):
                done(pe, "E_ahlow", g)
                split_product(pE[:, 0:D], [(*(t[:, c * D + side * P:c * D + (side + 1) * P] for t in E_ahl),
                                            *(w[:, c, (1 - side) * D:(2 - side) * D] for w in wij_hl))
                                           for c in range(K) for side in range(2)]).then_inc(S["E_m"], 1)

            def E_zT3(g):
                done(pe, "E_z3", g)
                transposes(pE[:, D:2 * D], E_z, K).then_inc(S["E_zT3"], 1)

            def E_h_step(g):
                done(pe, "E_hT3", g)
                project(pE[:, 0:F3 + 2], E_hT, w3_w).then_inc(S["E_h"], 1)

            def E_fT_step(g):
                done(pe, "E_fcopy", g)
                logits_transposed(pE[:, 256:384], E_f3).then_inc(S["E_fT"], 1)

            def E_s(g):
                done(pe, "E_fTc", g)
                one_head(pE[:, 384:512], E_fT, "E_s")

            def E_pT(g):
                done(pe, "E_exp", g)
                pe.transpose(pE[:, 256:384], E_l[:, :], ident[:, :]).then_inc(S["E_pT"], 1)

            def E_o(g):
                done(pe, "E_attn", g)
                pe.matmul(pE[:, 384:512], E_aT[:, :], E_h[:, 0:F3], start=True, stop=True).then_inc(S["E_o"], 1)

            rounds(pe, PE_ORDER, {
                "A_zT": A_zT, "A_f": A_f, "A_wh_hi": A_wh_hi, "A_wh_lo": A_wh_lo, "A_fT": A_fT_step, "A_s": A_s, "A_pT": A_pT,
                "B_o.0": B_o(0), "B_o": B_o(1), "B_wh.0": B_wh(0), "B_wh.1": B_wh(1), "B_wh.2": B_wh(2),
                "B_wh": B_wh(3),
                "C_fT": C_fT_step, "C_s": C_s, "C_pT": C_pT, "C_o": C_o, "C_hT": C_hT_step, "C_hid": C_hid_step,
                "C_ffn": C_ffn,
                "D_zT": D_zT, "D_q": D_q_step, "D_k.0": D_k_step, "D_kv": D_v_step, "F_s.0": F_s_step(0), "F_s": F_s_step(1),
                "F_pT.0": F_pT_step(0), "F_pT": F_pT_step(1), "F_o.0": F_o_step(0), "F_o": F_o_step(1),
                "F_oT": F_oT_step, "F_out": F_out,
                "E_ah": E_ah, "E_m": E_m, "E_zT3": E_zT3, "E_h": E_h_step, "E_fT": E_fT_step, "E_s": E_s,
                "E_pT": E_pT, "E_o": E_o,
            })


def kernel(**inputs):
    import numpy as np
    import concourse.bacc as bacc
    from concourse import mybir as mb
    from concourse.bass_utils import run_bass_kernel_spmd as run

    def transposed(a):
        return np.ascontiguousarray(np.asarray(a).T)

    def columns(a):
        return transposed(np.asarray(a).reshape(-1, 128))

    plain = lambda name: np.ascontiguousarray(np.asarray(inputs[name]))
    w_l2 = plain("L2_gnn_W")
    d = w_l2.shape[0]
    arrays = {
        "x": plain("x"), "adj": plain("adj"),
        "w_heads": plain("L0_gnn_W_heads"), "a_heads": plain("L0_gnn_a_heads"),
        "w_out": plain("L0_gnn_W_out"), "a_out": plain("L0_gnn_a_out"),
        "w1": plain("L0_gnn_w1"), "b1": columns(inputs["L0_gnn_b1"]), "w2": plain("L0_gnn_w2"), "b2": plain("L0_gnn_b2"),
        "gamma": plain("L0_gnn_ln_gamma"), "beta": plain("L0_gnn_ln_beta"),
        "wqT": transposed(inputs["L1_gnn_Wq"]), "bq": columns(inputs["L1_gnn_bq"]),
        "wkT": transposed(inputs["L1_gnn_Wk"]), "bk": columns(inputs["L1_gnn_bk"]),
        "wvT": transposed(inputs["L1_gnn_Wv"]), "bv": plain("L1_gnn_bv"),
        "woT": transposed(inputs["L1_gnn_Wo"]), "bo": plain("L1_gnn_bo"),
        "wijT": np.ascontiguousarray(np.concatenate([w_l2[:, :d].T, w_l2[:, d:].T], axis=1)),
        "b_l2": plain("L2_gnn_b"),
        "w_l3": plain("L3_gnn_W"), "a_l3": plain("L3_gnn_a"),
    }
    nc = bacc.Bacc("TRN2", target_bir_lowering=False, num_devices=1)
    args = [nc.dram_tensor(f"in_{n}", a.shape, mb.dt.from_np(a.dtype), kind="ExternalInput").ap()
            for n, a in arrays.items()]
    out = nc.dram_tensor("out_x", arrays["x"].shape, mb.dt.float32, kind="ExternalOutput").ap()
    gnn_stack(nc, *args, out)
    r = run(nc, [{f"in_{n}": a for n, a in arrays.items()}], core_ids=[0])
    return r.results[0]["out_x"]
```
